# Optimizing a Trainium2 kernel written in Bass

```python
import numpy as np
import jax
import jax.numpy as jnp

def _softmax(x, axis=-1):
    return jax.nn.softmax(x, axis=axis)

def _gelu(x):
    return jax.nn.gelu(x, approximate=True)

def _silu(x):
    return jax.nn.silu(x)

def _sigmoid(x):
    return jax.nn.sigmoid(x)

def _layernorm(x, axis=-1, eps=1e-05):
    m = jnp.mean(x, axis=axis, keepdims=True)
    v = jnp.var(x, axis=axis, keepdims=True)
    return (x - m) / jnp.sqrt(v + eps)

def _scatter_add(tgt, idx, src, axis=0):
    return tgt.at[idx].add(src)

def _segment_sum(src, seg, n):
    return jax.ops.segment_sum(src, seg, n)
kernel_name = 'mk_gnn_preln_d4_gnn_r32_1defdc'

def setup_inputs(seed: int=0):
    np.random.seed(seed)
    _w = jnp.asarray

    def _rec_inputs():
        import jax
        import jax.numpy as jnp
        _gk = jax.random.key(seed)
        x = -0.0005963 + 1.001 * jax.random.normal(jax.random.fold_in(_gk, 1), (96, 1024), jnp.float32)
        _s = jax.random.randint(jax.random.fold_in(_gk, 2), (768,), 0, 96, jnp.int32)
        _d = jax.random.randint(jax.random.fold_in(_gk, 3), (768,), 0, 96, jnp.int32)
        _loop = jnp.arange(96, dtype=jnp.int32)
        src = jnp.concatenate([_s, _d, _loop])
        dst = jnp.concatenate([_d, _s, _loop])
        _o = jnp.argsort(dst, stable=True)
        src = src[_o]
        dst = dst[_o]
        edge_type_5 = jax.random.randint(jax.random.fold_in(_gk, 13), (1632,), 0, 5, jnp.int32)
        return (x, src, dst, edge_type_5)
    x, src, dst, edge_type_5 = _rec_inputs()

    def _L0_gnn_setup():
        import jax, jax.numpy as jnp
        import numpy as np
        N = 96
        E = 3072
        IN_F = 1024
        OUT_F = 1024
        H = 16
        D = OUT_F // H
        NUM_ETYPES = 4

        def _build_mask(edge_index, edge_type, edge_type_weights, dtype):
            src, dst = (edge_index[0], edge_index[1])
            w = jax.nn.softplus(edge_type_weights)
            mask = jnp.full((N, N), -jnp.inf, dtype=dtype)
            mask = mask.at[src, dst].set(w[edge_type - 1])
            diag = jnp.diagonal(mask)
            idx = jnp.arange(N)
            mask = mask.at[idx, idx].set(jnp.where(jnp.isneginf(diag), w[3], diag))
            return mask
        key = jax.random.key(seed)
        ks = jax.random.split(key, 20)
        p = lambda k, shape: jax.random.normal(k, shape, dtype=jnp.float32) * 0.02
        return {'x': jax.random.normal(ks[0], (N, IN_F), dtype=jnp.float32), 'edge_index': jax.random.randint(ks[1], (2, E), 0, N), 'edge_type': jax.random.randint(ks[2], (E,), 1, NUM_ETYPES + 1), 'edge_type_weights': jnp.ones((NUM_ETYPES,), jnp.float32) + 0.1 * jax.random.normal(ks[3], (NUM_ETYPES,), dtype=jnp.float32), 'wq': p(ks[4], (OUT_F, IN_F)), 'bq': p(ks[5], (OUT_F,)), 'wk': p(ks[6], (OUT_F, IN_F)), 'bk': p(ks[7], (OUT_F,)), 'wv': p(ks[8], (OUT_F, IN_F)), 'bv': p(ks[9], (OUT_F,)), 'wiq': p(ks[10], (OUT_F, OUT_F)), 'biq': p(ks[11], (OUT_F,)), 'wik': p(ks[12], (OUT_F, OUT_F)), 'bik': p(ks[13], (OUT_F,)), 'wiv': p(ks[14], (OUT_F, OUT_F)), 'biv': p(ks[15], (OUT_F,)), 'wo': p(ks[16], (OUT_F, OUT_F)), 'bo': p(ks[17], (OUT_F,))}
    _L0_gnn_all = _L0_gnn_setup()
    _L0_gnn_in = {k: v for k, v in _L0_gnn_all.items() if k in ('edge_type_weights', 'wq', 'bq', 'wk', 'bk', 'wv', 'bv', 'wiq', 'biq', 'wik', 'bik', 'wiv', 'biv', 'wo', 'bo')}
    del _L0_gnn_all

    def _L1_gnn_setup():
        import jax, jax.numpy as jnp
        import numpy as np
        N_NODES = 25000
        N_EDGES = 12500
        D = 1024

        def _sage_layer(h, edge_src, edge_dst, deg_inv, W_self, W_neigh, b):
            msg = h[edge_src]
            agg = jax.ops.segment_sum(msg, edge_dst, num_segments=h.shape[0])
            mean = agg * deg_inv[:, None]
            return h @ W_self + mean @ W_neigh + b
        key = jax.random.key(seed)
        ks = jax.random.split(key, 8)
        s = 1.0 / np.sqrt(D)
        return {'x': jax.random.normal(ks[0], (N_NODES, D), dtype=jnp.float32), 'edge_src': jax.random.randint(ks[1], (N_EDGES,), 0, N_NODES, dtype=jnp.int32), 'edge_dst': jax.random.randint(ks[2], (N_EDGES,), 0, N_NODES, dtype=jnp.int32), 'W_self0': jax.random.normal(ks[3], (D, D), dtype=jnp.float32) * s, 'W_neigh0': jax.random.normal(ks[4], (D, D), dtype=jnp.float32) * s, 'b0': jnp.zeros((D,), dtype=jnp.float32), 'W_self1': jax.random.normal(ks[5], (D, D), dtype=jnp.float32) * s, 'W_neigh1': jax.random.normal(ks[6], (D, D), dtype=jnp.float32) * s, 'b1': jnp.zeros((D,), dtype=jnp.float32)}
    _L1_gnn_all = _L1_gnn_setup()
    _L1_gnn_in = {k: v for k, v in _L1_gnn_all.items() if k in ('W_self0', 'W_neigh0', 'b0', 'W_self1', 'W_neigh1', 'b1')}
    del _L1_gnn_all

    def _L2_gnn_setup():
        import jax, jax.numpy as jnp
        import numpy as np
        N = 625
        E = 10000
        D_IN = 1024
        D_OUT = 1024
        key = jax.random.key(seed)
        k1, k2, k3, k4 = jax.random.split(key, 4)
        x = jax.random.normal(k1, (N, D_IN), dtype=jnp.float32)
        edge_index = jax.random.randint(k2, (2, E), 0, N, dtype=jnp.int64)
        W = jax.random.normal(k3, (D_OUT, D_IN), dtype=jnp.float32) * (1.0 / np.sqrt(D_IN))
        b = jax.random.normal(k4, (D_OUT,), dtype=jnp.float32) * 0.01
        return {'x': x, 'edge_index': edge_index, 'W': W, 'b': b}
    _L2_gnn_all = _L2_gnn_setup()
    _L2_gnn_in = {k: v for k, v in _L2_gnn_all.items() if k in ('W', 'b')}
    del _L2_gnn_all

    def _L3_gnn_setup():
        import jax, jax.numpy as jnp
        import numpy as np
        N_NODES = 50000
        N_EDGES = 50000
        IN_DIM = 1024
        MID_DIM = 256

        def _gcn_conv(x, W, b, src, dst, norm, n):
            xw = x @ W
            msg = xw[src] * norm[:, None]
            out = jax.ops.segment_sum(msg, dst, num_segments=n)
            return out + b
        key = jax.random.key(seed)
        k1, k2, k3, k4 = jax.random.split(key, 4)
        x = jax.random.normal(k1, (N_NODES, IN_DIM), dtype=jnp.float32)
        edge_index = jax.random.randint(k2, (2, N_EDGES), 0, N_NODES, dtype=jnp.int64)
        W1 = jax.random.normal(k3, (IN_DIM, MID_DIM), dtype=jnp.float32) * (2.0 / (IN_DIM + MID_DIM)) ** 0.5
        W2 = jax.random.normal(k4, (MID_DIM, IN_DIM), dtype=jnp.float32) * (2.0 / (MID_DIM + IN_DIM)) ** 0.5
        b1 = jnp.zeros((MID_DIM,), dtype=jnp.float32)
        b2 = jnp.zeros((IN_DIM,), dtype=jnp.float32)
        return {'x': x, 'edge_index': edge_index, 'W1': W1, 'b1': b1, 'W2': W2, 'b2': b2}
    _L3_gnn_all = _L3_gnn_setup()
    _L3_gnn_in = {k: v for k, v in _L3_gnn_all.items() if k in ('W1', 'b1', 'W2', 'b2')}
    del _L3_gnn_all
    return {'x': x, 'src': src, 'dst': dst, 'edge_type_5': edge_type_5, 'L0_gnn_edge_type_weights': _L0_gnn_in['edge_type_weights'], 'L0_gnn_wq': _L0_gnn_in['wq'], 'L0_gnn_bq': _L0_gnn_in['bq'], 'L0_gnn_wk': _L0_gnn_in['wk'], 'L0_gnn_bk': _L0_gnn_in['bk'], 'L0_gnn_wv': _L0_gnn_in['wv'], 'L0_gnn_bv': _L0_gnn_in['bv'], 'L0_gnn_wiq': _L0_gnn_in['wiq'], 'L0_gnn_biq': _L0_gnn_in['biq'], 'L0_gnn_wik': _L0_gnn_in['wik'], 'L0_gnn_bik': _L0_gnn_in['bik'], 'L0_gnn_wiv': _L0_gnn_in['wiv'], 'L0_gnn_biv': _L0_gnn_in['biv'], 'L0_gnn_wo': _L0_gnn_in['wo'], 'L0_gnn_bo': _L0_gnn_in['bo'], 'L1_gnn_W_self0': _L1_gnn_in['W_self0'], 'L1_gnn_W_neigh0': _L1_gnn_in['W_neigh0'], 'L1_gnn_b0': _L1_gnn_in['b0'], 'L1_gnn_W_self1': _L1_gnn_in['W_self1'], 'L1_gnn_W_neigh1': _L1_gnn_in['W_neigh1'], 'L1_gnn_b1': _L1_gnn_in['b1'], 'L2_gnn_W': _L2_gnn_in['W'], 'L2_gnn_b': _L2_gnn_in['b'], 'L3_gnn_W1': _L3_gnn_in['W1'], 'L3_gnn_b1': _L3_gnn_in['b1'], 'L3_gnn_W2': _L3_gnn_in['W2'], 'L3_gnn_b2': _L3_gnn_in['b2']}

def reference(x, src, dst, edge_type_5, L0_gnn_edge_type_weights, L0_gnn_wq, L0_gnn_bq, L0_gnn_wk, L0_gnn_bk, L0_gnn_wv, L0_gnn_bv, L0_gnn_wiq, L0_gnn_biq, L0_gnn_wik, L0_gnn_bik, L0_gnn_wiv, L0_gnn_biv, L0_gnn_wo, L0_gnn_bo, L1_gnn_W_self0, L1_gnn_W_neigh0, L1_gnn_b0, L1_gnn_W_self1, L1_gnn_W_neigh1, L1_gnn_b1, L2_gnn_W, L2_gnn_b, L3_gnn_W1, L3_gnn_b1, L3_gnn_W2, L3_gnn_b2):
    import jax
    import jax.numpy as jnp

    def _L0_gnn_ref(x, edge_index, edge_type, edge_type_weights, wq, bq, wk, bk, wv, bv, wiq, biq, wik, bik, wiv, biv, wo, bo):
        import jax, jax.numpy as jnp
        import numpy as np
        N = 96
        E = 3072
        IN_F = 1024
        OUT_F = 1024
        H = 16
        D = OUT_F // H
        NUM_ETYPES = 4

        def _build_mask(edge_index, edge_type, edge_type_weights, dtype):
            src, dst = (edge_index[0], edge_index[1])
            w = jax.nn.softplus(edge_type_weights)
            mask = jnp.full((N, N), -jnp.inf, dtype=dtype)
            mask = mask.at[src, dst].set(w[edge_type - 1])
            diag = jnp.diagonal(mask)
            idx = jnp.arange(N)
            mask = mask.at[idx, idx].set(jnp.where(jnp.isneginf(diag), w[3], diag))
            return mask
        q = x @ wq.T + bq
        k = x @ wk.T + bk
        v = x @ wv.T + bv
        q2 = (q @ wiq.T + biq).reshape(N, H, D).transpose(1, 0, 2)
        k2 = (k @ wik.T + bik).reshape(N, H, D).transpose(1, 0, 2)
        v2 = (v @ wiv.T + biv).reshape(N, H, D).transpose(1, 0, 2)
        mask = _build_mask(edge_index, edge_type, edge_type_weights, x.dtype)
        scale = 1.0 / np.sqrt(D).astype(np.float32)
        scores = jnp.einsum('hnd,hmd->hnm', q2, k2) * scale + mask[None]
        attn = jax.nn.softmax(scores, axis=-1)
        out = jnp.einsum('hnm,hmd->hnd', attn, v2)
        out = out.transpose(1, 0, 2).reshape(N, OUT_F)
        return out @ wo.T + bo

    def _L1_gnn_ref(x, edge_src, edge_dst, W_self0, W_neigh0, b0, W_self1, W_neigh1, b1):
        import jax, jax.numpy as jnp
        import numpy as np
        N_NODES = 25000
        N_EDGES = 12500
        D = 1024

        def _sage_layer(h, edge_src, edge_dst, deg_inv, W_self, W_neigh, b):
            msg = h[edge_src]
            agg = jax.ops.segment_sum(msg, edge_dst, num_segments=h.shape[0])
            mean = agg * deg_inv[:, None]
            return h @ W_self + mean @ W_neigh + b
        N = x.shape[0]
        deg = jax.ops.segment_sum(jnp.ones_like(edge_dst, dtype=x.dtype), edge_dst, num_segments=N)
        deg_inv = 1.0 / jnp.maximum(deg, 1.0)
        h = jax.nn.relu(_sage_layer(x, edge_src, edge_dst, deg_inv, W_self0, W_neigh0, b0))
        out = _sage_layer(h, edge_src, edge_dst, deg_inv, W_self1, W_neigh1, b1)
        return out

    def _L2_gnn_ref(x, edge_index, W, b):
        import jax, jax.numpy as jnp
        import numpy as np
        N = 625
        E = 10000
        D_IN = 1024
        D_OUT = 1024
        num_nodes = x.shape[0]
        self_idx = jnp.arange(num_nodes, dtype=edge_index.dtype)
        ei = jnp.concatenate([edge_index, jnp.stack([self_idx, self_idx], axis=0)], axis=1)
        row, col = (ei[0], ei[1])
        h = jnp.einsum('nd,od->no', x, W) + b
        deg = jnp.zeros((num_nodes,), dtype=h.dtype).at[row].add(1.0)
        deg_inv_sqrt = deg ** (-0.5)
        norm = deg_inv_sqrt[row] * deg_inv_sqrt[col]
        msg = norm[:, None] * h[col]
        out = jax.ops.segment_sum(msg, row, num_segments=num_nodes)
        return out

    def _L3_gnn_ref(x, edge_index, W1, b1, W2, b2):
        import jax, jax.numpy as jnp
        import numpy as np
        N_NODES = 50000
        N_EDGES = 50000
        IN_DIM = 1024
        MID_DIM = 256

        def _gcn_conv(x, W, b, src, dst, norm, n):
            xw = x @ W
            msg = xw[src] * norm[:, None]
            out = jax.ops.segment_sum(msg, dst, num_segments=n)
            return out + b
        n = x.shape[0]
        loops = jnp.arange(n, dtype=edge_index.dtype)
        src = jnp.concatenate([edge_index[0], loops])
        dst = jnp.concatenate([edge_index[1], loops])
        deg = jax.ops.segment_sum(jnp.ones_like(dst, dtype=x.dtype), dst, num_segments=n)
        dis = jnp.where(deg > 0, jax.lax.rsqrt(jnp.maximum(deg, 1.0)), 0.0)
        norm = dis[src] * dis[dst]
        h = jax.nn.relu(_gcn_conv(x, W1, b1, src, dst, norm, n))
        out = _gcn_conv(h, W2, b2, src, dst, norm, n)
        return out
    edge_index = jnp.stack([src, dst])
    h = jnp.maximum(_layernorm(x, axis=-1), 0.0)
    x = x + _L0_gnn_ref(h, edge_index, edge_type_5, L0_gnn_edge_type_weights, L0_gnn_wq, L0_gnn_bq, L0_gnn_wk, L0_gnn_bk, L0_gnn_wv, L0_gnn_bv, L0_gnn_wiq, L0_gnn_biq, L0_gnn_wik, L0_gnn_bik, L0_gnn_wiv, L0_gnn_biv, L0_gnn_wo, L0_gnn_bo)
    h = jnp.maximum(_layernorm(x, axis=-1), 0.0)
    x = x + _L1_gnn_ref(h, src, dst, L1_gnn_W_self0, L1_gnn_W_neigh0, L1_gnn_b0, L1_gnn_W_self1, L1_gnn_W_neigh1, L1_gnn_b1)
    h = jnp.maximum(_layernorm(x, axis=-1), 0.0)
    x = x + _L2_gnn_ref(h, edge_index, L2_gnn_W, L2_gnn_b)
    h = jnp.maximum(_layernorm(x, axis=-1), 0.0)
    x = x + _L3_gnn_ref(h, edge_index, L3_gnn_W1, L3_gnn_b1, L3_gnn_W2, L3_gnn_b2)
    return x

_drawn_inputs = setup_inputs


def setup_inputs(seed=0):
    import zlib

    import numpy as np

    out = dict(_drawn_inputs(seed))
    spreads = {'L1_gnn_b0': (0.0, 0.1),
     'L1_gnn_b1': (0.0, 0.1),
     'L3_gnn_b1': (0.0, 0.1),
     'L3_gnn_b2': (0.0, 0.1)}
    factors = {'L0_gnn_edge_type_weights': 64.0,
     'L0_gnn_wq': 8.0,
     'L0_gnn_bq': 8.0,
     'L0_gnn_wk': 8.0,
     'L0_gnn_bk': 64.0,
     'L0_gnn_bv': 7.5,
     'L0_gnn_wiq': 8.0,
     'L0_gnn_biq': 64.0,
     'L0_gnn_wik': 8.0,
     'L0_gnn_bik': 64.0,
     'L0_gnn_biv': 4.726,
     'L0_gnn_bo': 2.949,
     'L2_gnn_b': 8.0}
    for name, (base, spread) in spreads.items():
        noise = np.random.default_rng([zlib.crc32(name.encode()), seed]).standard_normal(out[name].shape)
        drawn = base * np.exp(spread * noise) if base else spread * noise
        out[name] = jnp.asarray(drawn.astype(out[name].dtype))
    for name, factor in factors.items():
        out[name] = (out[name] * factor).astype(out[name].dtype)
    return out
```

```python
import concourse.bass as bass
from concourse import mybir
from contextlib import ExitStack

N, D, F = 96, 1024, 256
P = 128
KC = D // P
H, DH = 16, 64
NE, EC = 1632, 17
HB = D // 2
HC = KC // 2
TW = HC * N
LN_EPS = 1e-5
SCALE = 1.0 / DH ** 0.5
NO_EDGE = -1.0e30
TRI = 32768.0
UNITS, UNIT = 50, 2 * D
RAW, RING = 5, 10
DIRECT_UNITS = (20, 21, 22)

Q, K, V, Q2, K2, V2, O, SAGE0, SAGE1, GCN2, GCN3A, GCN3B = range(12)
FIRST_UNIT = {Q: 0, K: 4, V: 8, Q2: 12, K2: 16, V2: 20, O: 24, SAGE0: 28, SAGE1: 36, GCN2: 44, GCN3A: 48, GCN3B: 49}

SPLIT = [g for g in range(2 * UNITS) if g // 2 not in DIRECT_UNITS]
PLACE = {g: s for s, g in enumerate(SPLIT)}
BEFORE = {i: sum(g < 2 * u for g in SPLIT) for i, u in FIRST_UNIT.items()}

EVENTS = [("h0T", 2), ("qT", 2), ("eqA", 2), ("eqB", 2), ("kT", 2), ("keyA", 2), ("keyB", 2), ("vT", 2), ("counts", 1),
          ("degrees", 1), ("q2T", 2), ("k2T", 2), ("scores0", 2), ("scores1", 2), ("probsT0", 2), ("probsT1", 2),
          ("headsT", 2), ("h1T", 2), ("mean1T", 2), ("rowsum", 1), ("hiddenT", 2), ("mean2T", 2), ("h2T", 2),
          ("h3T", 2), ("gT", 1)]


def bank_fills():
    count, out = [0] * 8, {}
    for t, (name, halves) in enumerate(EVENTS):
        for j in range(halves):
            b = 4 + 2 * (t % 2) + j
            count[b] += 1
            out[name, j] = (b, count[b])
    return out


FILL = bank_fills()
for _i in range(12):
    for _j in range(2):
        FILL[_i, _j] = (2 * (_i % 2) + _j, _i // 2 + 1)

PIECES = [(0, 5), (5, 9), (9, 13), (13, 17)]
ACT_HI = ["h0T", "qT", "kT", "vT", "headsT", "h1T", "mean1T", "hiddenT", "mean2T", "h2T", "h3T", "gT"]
HI_COUNT = {}
for _name in ACT_HI:
    for _j in range(1 if _name == "gT" else 2):
        HI_COUNT[_name, _j] = len(HI_COUNT) + 1


def gnn_kernel(nc, x_in, weights, biases, edges, edge_w, out):
    f32, f32r, bf16, i32 = mybir.dt.float32, mybir.dt.float32r, mybir.dt.bfloat16, mybir.dt.int32
    ALU, ACT, AX = mybir.AluOpType, mybir.ActivationFunctionType, mybir.AxisListType
    ctx = ExitStack()
    with ctx:
        def sb(name, shape, dt=f32):
            return ctx.enter_context(nc.sbuf_tensor(name, shape, dt))

        def sem(name):
            return ctx.enter_context(nc.semaphore(name))

        raw = sb("raw", [P, RAW, 2, D])
        w_hi = sb("w_hi", [P, RING, D], f32r)
        w_lo = sb("w_lo", [P, RING, D], f32r)
        x = sb("x", [N, D])
        h = sb("h", [N, D])
        ev = sb("ev", [N, 2, D])
        a_hi = sb("a_hi", [P, 3, KC, N], f32r)
        a_lo = sb("a_lo", [P, 3, KC, N], f32r)
        vT = sb("vT", [P, KC, N])
        q2T = sb("q2T", [P, KC, N])
        k2T = sb("k2T", [P, KC, N])
        S = sb("S", [N, EC, N])
        PT = sb("PT", [N, EC, N])
        onehot = PT[:, :, :].rearrange("p c n -> p (c n)").bitcast(bf16).rearrange("p (k c n) -> p k c n", k=2, c=EC)
        oh_src, oh_dst = onehot[:, 0], onehot[:, 1]
        diag = S
        oh_key = sb("oh_key", [N, EC, N], bf16)
        same = sb("same", [N, 5, N], bf16)
        b_hi = sb("b_hi", [12, D], f32r)
        b_lo = sb("b_lo", [12, D], f32r)
        b_raw = ev[0:12, 1, :]
        sel = sb("sel", [12, 12, N], f32r)
        sel_f = S[0:12, 0:12, :]
        rs_hi = sb("rs_hi", [12, N], f32r)
        rs_lo = sb("rs_lo", [12, N], f32r)
        ident = sb("ident", [N, N])
        ident_b = sb("ident_b", [N, N], bf16)
        ones = sb("ones", [N, N])
        tri_b = sb("tri_b", [N, N], bf16)
        iota_i = sb("iota_i", [N, N], i32)
        iota_f = sb("iota_f", [N, N])
        bcol = sb("bcol", [N, 12])
        edges_i = sb("edges_i", [N, 3, EC], i32)
        edges_f = sb("edges_f", [N, 3, EC])
        src, dst, typ = (edges_f[:, n, :] for n in range(3))
        pair = sb("pair", [N, EC])
        key_i = sb("key_i", [N, EC], i32)
        key = sb("key", [N, EC])
        dup = sb("dup", [N, EC])
        kmax = sb("kmax", [N, 4, N])
        kind_i = sb("kind_i", [N, 2, N], i32)
        kind = sb("kind", [N, N])
        mterm = sb("mterm", [N, 3, N])
        mask = sb("mask", [N, N])
        ew = sb("ew", [N, 4])
        ews = sb("ews", [N, 4, 4])
        C = sb("C", [N, 2, N])
        deg = sb("deg", [N, 2 * N + 2])
        dis = sb("dis", [N, 2, 2 * N + 2])
        mdeg = sb("mdeg", [N, 2, N])
        A1T = sb("A1T", [N, N])
        A2T = sb("A2T", [N, N])
        A3T = sb("A3T", [N, N])
        atmp = sb("atmp", [N, 4, N])
        stats = sb("stats", [N, 2, 6])
        mv = sb("mv", [N, 2])
        lnc = sb("lnc", [N, 3])
        nmax = sb("nmax", [N, 2, H])
        rsum = sb("rsum", [N, 2, H])
        psum = [ctx.enter_context(nc.psum_tensor(f"bank{b}", [P, HB], f32)) for b in range(8)]

        x_loaded = [sem(f"x_loaded{j}") for j in range(2)]
        edges_loaded, biases_loaded, ew_loaded = sem("edges_loaded"), sem("biases_loaded"), sem("ew_loaded")
        raw_loaded = [sem(f"raw_loaded{r}") for r in range(RAW)]
        raw_used = [sem(f"raw_used{r}") for r in range(RAW)]
        hi_ready = sem("hi_ready")
        ring_free = sem("ring_free")
        full = [sem(f"full{b}") for b in range(8)]
        drained = [sem(f"drained{b}") for b in range(8)]
        act_hi = sem("act_hi")
        normed = sem("normed")
        var_ready, std_ready, coef_ready = sem("var_ready"), sem("std_ready"), sem("coef_ready")
        bias_hi, bias_lo, sel_ready, ident_ready = sem("bias_hi"), sem("bias_lo"), sem("sel_ready"), sem("ident_ready")
        diag_ready, dup_ready, onehots_ready, keys_ready = sem("diag_ready"), sem("dup_ready"), sem("onehots_ready"), sem("keys_ready")
        kind_ready, ew_ready, mask_ready = sem("kind_ready"), sem("ew_ready"), sem("mask_ready")
        mdeg_ready, sdeg_ready, dis_ready = sem("mdeg_ready"), sem("sdeg_ready"), sem("dis_ready")
        A1_ready, A23_ready = sem("A1_ready"), sem("A23_ready")
        max_ready, exp_ready, probs_ready = sem("max_ready"), sem("exp_ready"), sem("probs_ready")
        pool_step, dve_step, act_step = sem("pool_step"), sem("dve_step"), sem("act_step")
        out_ready, stored = sem("out_ready"), sem("stored")

        def tcols(j):
            return slice(j * HC, (j + 1) * HC)

        def hcols(j):
            return slice(j * HB, (j + 1) * HB)

        def tview(b, rows=P, k=HC):
            return psum[b][0:rows, 0:k * N].rearrange("p (c n) -> p c n", n=N)

        block = ctx.enter_context(nc.Block())

        @block.sync
        def _(sp):
            for j in range(2):
                sp.dma_start(x[:, hcols(j)], x_in[:, hcols(j)]).then_inc(x_loaded[j], 16)

            def load(u, r):
                sp.dma_start(raw[:, r, :, :].rearrange("p c n -> p (c n)"), weights[u]).then_inc(raw_loaded[r], 16)

            for r in range(RAW):
                load(r, r)
            with sp.Fori(1, UNITS // RAW) as turn:
                for r in range(RAW):
                    sp.wait_ge(raw_used[r], turn * 2)
                    load(turn * RAW + r, r)
            for j in range(2):
                sp.wait_ge(out_ready, j + 1)
                sp.dma_start(out[:, hcols(j)], x[:, hcols(j)]).then_inc(stored, 16)
            sp.wait_ge(stored, 32)

        @block.gpsimd
        def _(pool):
            steps = [0]

            def step(ins):
                steps[0] += 1
                ins.then_inc(pool_step, 1)
                pool.wait_ge(pool_step, steps[0])

            g = nc.gpsimd
            step(g.memset(ident[:, :], 0.0))
            g.affine_select(out=ident[:, :], in_=ident[:, :], compare_op=ALU.not_equal, fill=1.0, base=0,
                            pattern=[[-1, N]], channel_multiplier=1).then_inc(ident_ready, 1)
            step(g.memset(sel_f, 0.0))
            step(g.affine_select(out=sel_f, in_=sel_f, compare_op=ALU.not_equal, fill=1.0, base=0,
                                 pattern=[[1, 12], [0, N]], channel_multiplier=-1))
            g.tensor_copy(sel[:, :, :], sel_f).then_inc(sel_ready, 1)
            pool.wait_ge(ident_ready, 1)
            step(g.tensor_copy(ident_b[:, :], ident[:, :]))
            step(g.memset(ones[:, :], 1.0))
            step(g.affine_select(out=tri_b[:, :], in_=ones[:, :], compare_op=ALU.is_ge, fill=0.0, base=0,
                                 pattern=[[-1, N]], channel_multiplier=1))
            step(g.tensor_scalar(tri_b[:, :], tri_b[:, :], TRI, 1.0, ALU.mult, ALU.mult))
            step(g.memset(bcol[:, :], 0.0))
            step(g.memset(bcol[:, GCN2:GCN2 + 1], 1.0))
            step(g.iota(iota_i[:, :], [[1, N]], base=0, channel_multiplier=0))
            step(g.tensor_copy(iota_f[:, :], iota_i[:, :]))
            step(g.iota(key_i[:, :], [[8, EC]], base=1, channel_multiplier=0))
            step(g.tensor_copy(key[:, :], key_i[:, :]))
            pool.wait_ge(edges_loaded, 16)
            step(g.tensor_copy(edges_f[:, :, :], edges_i[:, :, :]))
            step(g.tensor_scalar(pair[:, :], src, float(N), 0.0, ALU.mult, ALU.add))
            step(g.tensor_tensor(pair[:, :], pair[:, :], dst, ALU.add))
            step(g.tensor_tensor(key[:, :], key[:, :], typ, ALU.add))
            pool.wait_ge(sel_ready, 1)
            g.tensor_tensor(diag[:, :, :], ident[:, :].unsqueeze(1).to_broadcast([N, EC, N]),
                            pair[:, :].unsqueeze(2).to_broadcast([N, EC, N]), ALU.mult).then_inc(diag_ready, 1)
            for c in range(EC):
                g.tensor_scalar(oh_src[:, c, :], iota_f[:, :], src[:, c:c + 1], None, ALU.is_equal)\
                    .then_inc(onehots_ready, 1)
                g.tensor_scalar(oh_dst[:, c, :], iota_f[:, :], dst[:, c:c + 1], None, ALU.is_equal)\
                    .then_inc(onehots_ready, 1)
            pool.wait_ge(dup_ready, 4)
            step(g.tensor_scalar(dup[:, :], dup[:, :], -1.0, 1.0, ALU.mult, ALU.add))
            step(g.tensor_tensor(key[:, :], key[:, :], dup[:, :], ALU.mult))
            for c in range(EC):
                g.tensor_scalar(oh_key[:, c, :], iota_f[:, :], dst[:, c:c + 1], key[:, c:c + 1], ALU.is_equal, ALU.mult)\
                    .then_inc(keys_ready, 1)
            pool.wait_ge(kind_ready, 1)
            pool.wait_ge(ew_ready, 1)
            none, off, on = (mterm[:, n, :] for n in range(3))
            w = ews[:, 3, :]
            step(g.tensor_scalar(none, kind[:, :], 0.0, None, ALU.is_equal))
            step(g.tensor_tensor(on, none, ident[:, :], ALU.mult))
            step(g.tensor_tensor(off, none, on, ALU.subtract))
            step(g.tensor_scalar(off, off, NO_EDGE, 0.0, ALU.mult, ALU.add))
            step(g.tensor_scalar(on, on, w[:, 3:4], 0.0, ALU.mult, ALU.add))
            step(g.tensor_tensor(mask[:, :], off, on, ALU.add))
            for k, m in ((1, 3), (2, 0), (3, 1), (4, 2), (5, 3)):
                step(g.tensor_scalar(on, kind[:, :], float(k), w[:, m:m + 1], ALU.is_equal, ALU.mult))
                ins = g.tensor_tensor(mask[:, :], mask[:, :], on, ALU.add)
                if k < 5:
                    step(ins)
                else:
                    ins.then_inc(mask_ready, 1)
            pool.wait_ge(mdeg_ready, 1)
            g.tensor_tensor(A1T[:, :], C[:, 0, :], mdeg[:, 1, :], ALU.mult).then_inc(A1_ready, 1)
            pool.wait_ge(dis_ready, 1)
            for k, (cc, AT) in enumerate(((1, A2T), (0, A3T))):
                by = 1 - k
                step(g.tensor_tensor(atmp[:, 2 * k, :], C[:, cc, :], ident[:, :], ALU.add))
                step(g.tensor_tensor(atmp[:, 2 * k + 1, :], atmp[:, 2 * k, :], dis[:, 1, by * N:(by + 1) * N], ALU.mult))
                g.tensor_scalar(AT[:, :], atmp[:, 2 * k + 1, :], dis[:, 1, 2 * N + by:2 * N + by + 1], 0.0,
                                ALU.mult, ALU.add).then_inc(A23_ready, 1)

        @block.scalar
        def _(act):
            a = nc.scalar
            steps, done = [0], [0]

            def step(ins):
                steps[0] += 1
                ins.then_inc(act_step, 1)
                act.wait_ge(act_step, steps[0])

            def weights_hi(upto):
                while done[0] < min(upto, len(SPLIT)):
                    s = done[0]
                    u, c = divmod(SPLIT[s], 2)
                    if c == 0 or s == 0:
                        act.wait_ge(raw_loaded[u % RAW], 16 * (u // RAW + 1))
                    if s >= RING:
                        act.wait_ge(ring_free, s - RING + 1)
                    a.activation(w_hi[:, s % RING, :], raw[:, u % RAW, c, :], ACT.Copy).then_inc(hi_ready, 1)
                    done[0] += 1

            def wait_full(key):
                b, n = FILL[key]
                act.wait_ge(full[b], n)
                return b

            def copy_out(i, j, func=ACT.Copy, cols=HB):
                b = wait_full((i, j))
                a.activation(ev[:, i % 2, j * HB:j * HB + cols], psum[b][0:N, 0:cols], func).then_inc(drained[b], 1)

            def acts_hi(name, slot, halves=2, k=HC):
                for j in range(halves):
                    b = wait_full((name, j))
                    a.activation(a_hi[:, slot, j * HC:j * HC + k, :], tview(b, k=k), ACT.Copy).then_inc(act_hi, 1)

            def transposed_out(name, j, tile):
                b = wait_full((name, j))
                a.activation(tile[:, tcols(j), :], tview(b), ACT.Copy).then_inc(drained[b], 1)

            def norm(layer):
                act.wait_ge(var_ready, layer + 1)
                a.activation(lnc[:, 0:1], mv[:, 1:2], ACT.Sqrt).then_inc(std_ready, 1)
                act.wait_ge(coef_ready, layer + 1)
                for j in range(2):
                    a.activation(h[:, hcols(j)], x[:, hcols(j)], ACT.Relu, bias=lnc[:, 2:3], scale=lnc[:, 1:2])\
                        .then_inc(normed, 1)

            act.dma_start(edges_i[:, :, :], edges).then_inc(edges_loaded, 16)
            act.dma_start(b_raw, biases).then_inc(biases_loaded, 16)
            act.dma_start(ew[:, :], edge_w.to_broadcast([N, 4])).then_inc(ew_loaded, 16)
            norm(0)
            act.wait_ge(biases_loaded, 16)
            a.activation(b_hi[:, :], b_raw, ACT.Copy).then_inc(bias_hi, 1)
            acts_hi("h0T", 0)
            weights_hi(BEFORE[K] + 2)
            copy_out(Q, 0)
            weights_hi(BEFORE[K] + 4)
            acts_hi("qT", 1)
            weights_hi(BEFORE[V] + 2)
            copy_out(K, 0)
            weights_hi(BEFORE[V] + 4)
            acts_hi("kT", 2)
            weights_hi(BEFORE[Q2] + 1)
            copy_out(V, 0)
            weights_hi(BEFORE[Q2] + 3)
            b = wait_full(("vT", 0))
            a.activation(vT[:, 0:4, :], tview(b), ACT.Copy).then_inc(drained[b], 1)
            b = wait_full(("vT", 1))
            step(a.activation(vT[:, 4:6, :], tview(b)[:, 0:2, :], ACT.Copy))
            a.activation(a_hi[:, 0, 6:8, :], tview(b)[:, 2:4, :], ACT.Copy).then_inc(act_hi, 2)
            act.wait_ge(ew_loaded, 16)
            step(a.activation(ews[:, 0, :], ew[:, :], ACT.Abs))
            step(a.activation(ews[:, 1, :], ews[:, 0, :], ACT.Exp, scale=-1.0))
            step(a.activation(ews[:, 2, :], ews[:, 1, :], ACT.Ln, bias=1.0))
            weights_hi(BEFORE[K2] + 1)
            copy_out(Q2, 0)
            weights_hi(BEFORE[K2] + 4)
            transposed_out("q2T", 0, q2T)
            weights_hi(BEFORE[V2])
            copy_out(K2, 0)
            transposed_out("k2T", 0, k2T)
            weights_hi(BEFORE[V2] + 1)
            for p in range(4):
                act.wait_ge(max_ready, p + 1)
                for hh in range(4 * p, 4 * p + 4):
                    ins = a.activation(S[:, hh, :], S[:, hh, :], ACT.Exp, bias=nmax[:, 1, hh:hh + 1],
                                       accum_out=rsum[:, 0, hh:hh + 1])
                    ins.then_inc(exp_ready, 1)
            weights_hi(BEFORE[O])
            copy_out(V2, 0)
            for p in (0, 2):
                b = wait_full((f"probsT{p // 2}", p % 2))
                a.activation(PT[:, 4 * p:4 * p + 4, :], tview(b, N), ACT.Copy).then_inc(drained[b], 1)
            acts_hi("headsT", 1)
            weights_hi(BEFORE[SAGE0])
            norm(1)
            weights_hi(BEFORE[SAGE0] + 1)
            acts_hi("h1T", 2)
            acts_hi("mean1T", 0)
            b, n = FILL["degrees", 0]
            act.wait_ge(drained[b], n)
            a.activation(dis[:, 0, :], deg[:, :], ACT.Sqrt).then_inc(sdeg_ready, 1)
            weights_hi(BEFORE[SAGE1])
            copy_out(SAGE0, 0, ACT.Relu)
            weights_hi(BEFORE[SAGE1] + 1)
            acts_hi("hiddenT", 1)
            acts_hi("mean2T", 2)
            weights_hi(BEFORE[GCN2])
            norm(2)
            weights_hi(BEFORE[GCN2] + 1)
            acts_hi("h2T", 0)
            weights_hi(BEFORE[GCN3A])
            norm(3)
            acts_hi("h3T", 1)
            weights_hi(len(SPLIT))
            copy_out(GCN3A, 0, ACT.Relu, F)
            acts_hi("gT", 2, 1, 2)

        @block.vector
        def _(dve):
            v = nc.vector
            steps, done = [0], [0]

            def step(ins):
                steps[0] += 1
                ins.then_inc(dve_step, 1)
                dve.wait_ge(dve_step, steps[0])

            def weights_lo(upto):
                while done[0] < min(upto, len(SPLIT)):
                    s = done[0]
                    u, c = divmod(SPLIT[s], 2)
                    dve.wait_ge(hi_ready, s + 1)
                    v.tensor_tensor(w_lo[:, s % RING, :], raw[:, u % RAW, c, :], w_hi[:, s % RING, :].bitcast(f32),
                                    ALU.subtract).then_inc(raw_used[u % RAW], 1)
                    done[0] += 1

            def wait_full(key):
                b, n = FILL[key]
                dve.wait_ge(full[b], n)
                return b

            def copy_out(i, j):
                b = wait_full((i, j))
                v.tensor_copy(ev[:, i % 2, hcols(j)], psum[b][0:N, :]).then_inc(drained[b], 1)

            def acts_lo(name, slot, halves=2, k=HC):
                for j in range(halves):
                    b, _ = FILL[name, j]
                    dve.wait_ge(act_hi, HI_COUNT[name, j])
                    v.tensor_tensor(a_lo[:, slot, j * HC:j * HC + k, :], tview(b, k=k),
                                    a_hi[:, slot, j * HC:j * HC + k, :].bitcast(f32), ALU.subtract)\
                        .then_inc(drained[b], 1)

            def transposed_out(name, j, tile):
                b = wait_full((name, j))
                v.tensor_copy(tile[:, tcols(j), :], tview(b)).then_inc(drained[b], 1)

            def residual(i):
                for j in range(2):
                    b = wait_full((i, j))
                    v.tensor_tensor(x[:, hcols(j)], psum[b][0:N, :], x[:, hcols(j)], ALU.add).then_inc(drained[b], 1)
                    dve.wait_ge(drained[b], FILL[i, j][1])
                    ins = v.bn_stats(stats[:, j, :], x[:, hcols(j)])
                    if j == 1:
                        step(ins)
                    else:
                        ins.then_inc(dve_step, 1)
                        steps[0] += 1

            def norm(layer):
                step(v.bn_aggr(mv[:, :], stats[:, :, :].rearrange("p a b -> p (a b)")))
                v.tensor_scalar(mv[:, 1:2], mv[:, 1:2], LN_EPS, None, ALU.add).then_inc(var_ready, 1)
                dve.wait_ge(std_ready, layer + 1)
                step(v.reciprocal(lnc[:, 1:2], lnc[:, 0:1]))
                v.scalar_tensor_tensor(lnc[:, 2:3], mv[:, 0:1], -1.0, lnc[:, 1:2], ALU.mult, ALU.mult)\
                    .then_inc(coef_ready, 1)

            for j in range(2):
                dve.wait_ge(x_loaded[j], 16)
                step(v.bn_stats(stats[:, j, :], x[:, hcols(j)]))
            norm(0)
            dve.wait_ge(bias_hi, 1)
            v.tensor_tensor(b_lo[:, :], b_raw, b_hi[:, :].bitcast(f32), ALU.subtract).then_inc(bias_lo, 1)
            acts_lo("h0T", 0)
            weights_lo(BEFORE[K] + 2)
            dve.wait_ge(bias_lo, 1)
            copy_out(Q, 1)
            weights_lo(BEFORE[K] + 4)
            acts_lo("qT", 1)

            def mark_voids(p):
                c0, c1 = PIECES[p]
                b = wait_full((("eqA", "eqB")[p // 2], p % 2))
                v.tensor_tensor(same[:, 0:c1 - c0, :], tview(b, N, c1 - c0),
                                pair[:, c0:c1].unsqueeze(2).to_broadcast([N, c1 - c0, N]), ALU.is_equal)\
                    .then_inc(drained[b], 1)
                dve.wait_ge(drained[b], FILL[(("eqA", "eqB")[p // 2], p % 2)][1])
                v.reduce_max(dup[:, c0:c1], same[:, 0:c1 - c0, :], AX.X).then_inc(dup_ready, 1)
                dve.wait_ge(dup_ready, p + 1)

            weights_lo(BEFORE[K] + 5)
            dve.wait_ge(diag_ready, 1)
            mark_voids(0)
            mark_voids(1)
            weights_lo(BEFORE[K] + 7)
            mark_voids(2)
            mark_voids(3)
            weights_lo(BEFORE[V] + 2)
            copy_out(K, 1)
            weights_lo(BEFORE[V] + 4)
            acts_lo("kT", 2)

            def last_keys(p):
                c0, c1 = PIECES[p]
                b = wait_full((("keyA", "keyB")[p // 2], p % 2))
                v.tensor_reduce(out=kmax[:, p, :], in_=tview(b, N, c1 - c0).rearrange("p c d -> p d c"), axis=AX.X,
                                op=ALU.max).then_inc(drained[b], 1)

            weights_lo(BEFORE[V] + 6)
            last_keys(0)
            last_keys(1)
            weights_lo(BEFORE[V] + 7)
            last_keys(2)
            last_keys(3)
            for p in range(4):
                b, n = FILL[("keyA", "keyB")[p // 2], p % 2]
                dve.wait_ge(drained[b], n)
            weights_lo(BEFORE[Q2] + 1)
            copy_out(V, 1)
            step(v.tensor_tensor(kmax[:, 0:2, :], kmax[:, 0:2, :], kmax[:, 2:4, :], ALU.max))
            step(v.tensor_tensor(kmax[:, 0, :], kmax[:, 0, :], kmax[:, 1, :], ALU.max))
            step(v.tensor_copy(kind_i[:, 0, :], kmax[:, 0, :]))
            step(v.tensor_scalar(kind_i[:, 1, :], kind_i[:, 0, :], 7, None, ALU.bitwise_and))
            v.tensor_copy(kind[:, :], kind_i[:, 1, :]).then_inc(kind_ready, 1)
            weights_lo(BEFORE[Q2] + 3)
            b, _ = FILL["vT", 1]
            dve.wait_ge(act_hi, HI_COUNT["vT", 1])
            v.tensor_tensor(a_lo[:, 0, 6:8, :], tview(b)[:, 2:4, :], a_hi[:, 0, 6:8, :].bitcast(f32), ALU.subtract)\
                .then_inc(drained[b], 1)
            dve.wait_ge(act_step, 4)
            v.scalar_tensor_tensor(ews[:, 3, :], ew[:, :], 0.0, ews[:, 2, :], ALU.max, ALU.add).then_inc(ew_ready, 1)
            weights_lo(BEFORE[Q2] + 6)
            b = wait_full(("counts", 0))
            v.tensor_copy(C[:, :, :], tview(b, N, 2)).then_inc(drained[b], 1)
            weights_lo(BEFORE[K2] + 1)
            copy_out(Q2, 1)
            weights_lo(BEFORE[K2] + 2)
            b = wait_full(("degrees", 0))
            step(v.tensor_scalar(mdeg[:, 0, :], psum[b][0:N, 0:N], 1.0, None, ALU.max))
            v.reciprocal(mdeg[:, 1, :], mdeg[:, 0, :]).then_inc(mdeg_ready, 1)
            v.tensor_scalar(deg[:, :], psum[b][0:N, 0:2 * N + 2], 1.0, None, ALU.add).then_inc(drained[b], 1)
            weights_lo(BEFORE[K2] + 4)
            transposed_out("q2T", 1, q2T)
            weights_lo(BEFORE[V2])
            copy_out(K2, 1)
            transposed_out("k2T", 1, k2T)
            weights_lo(BEFORE[V2] + 1)
            dve.wait_ge(mask_ready, 1)
            for p in range(4):
                name = f"scores{p // 2}"
                b = wait_full((name, p % 2))
                heads = slice(4 * p, 4 * p + 4)
                v.scalar_tensor_tensor(S[:, heads, :], tview(b, N), SCALE,
                                       mask[:, :].unsqueeze(1).to_broadcast([N, 4, N]), ALU.mult, ALU.add)\
                    .then_inc(drained[b], 1)
                dve.wait_ge(drained[b], FILL[name, p % 2][1])
                step(v.reduce_max(nmax[:, 0, heads], S[:, heads, :], AX.X))
                v.tensor_scalar(nmax[:, 1, heads], nmax[:, 0, heads], -1.0, None, ALU.mult).then_inc(max_ready, 1)
            for p in range(4):
                heads = slice(4 * p, 4 * p + 4)
                dve.wait_ge(exp_ready, 4 * p + 4)
                step(v.reciprocal(rsum[:, 1, heads], rsum[:, 0, heads]))
                v.tensor_tensor(S[:, heads, :], S[:, heads, :],
                                rsum[:, 1, heads].unsqueeze(2).to_broadcast([N, 4, N]), ALU.mult)\
                    .then_inc(probs_ready, 1)
            weights_lo(BEFORE[O])
            copy_out(V2, 1)
            for p in (1, 3):
                b = wait_full((f"probsT{p // 2}", p % 2))
                v.tensor_copy(PT[:, 4 * p:4 * p + 4, :], tview(b, N)).then_inc(drained[b], 1)
            acts_lo("headsT", 1)
            weights_lo(BEFORE[SAGE0])
            residual(O)
            norm(1)
            weights_lo(BEFORE[SAGE0] + 1)
            acts_lo("h1T", 2)
            acts_lo("mean1T", 0)
            dve.wait_ge(sdeg_ready, 1)
            v.reciprocal(dis[:, 1, :], dis[:, 0, :]).then_inc(dis_ready, 1)
            weights_lo(BEFORE[SAGE0] + 6)
            b = wait_full(("rowsum", 0))
            step(v.tensor_copy(rs_hi[:, :], psum[b][0:12, 0:N]))
            v.tensor_tensor(rs_lo[:, :], psum[b][0:12, 0:N], rs_hi[:, :].bitcast(f32), ALU.subtract)\
                .then_inc(drained[b], 1)
            weights_lo(BEFORE[SAGE1])
            b = wait_full((SAGE0, 1))
            v.tensor_scalar(ev[:, SAGE0 % 2, hcols(1)], psum[b][0:N, :], 0.0, None, ALU.max).then_inc(drained[b], 1)
            weights_lo(BEFORE[SAGE1] + 1)
            acts_lo("hiddenT", 1)
            acts_lo("mean2T", 2)
            weights_lo(BEFORE[GCN2])
            residual(SAGE1)
            norm(2)
            weights_lo(BEFORE[GCN2] + 1)
            acts_lo("h2T", 0)
            weights_lo(BEFORE[GCN3A])
            residual(GCN2)
            norm(3)
            acts_lo("h3T", 1)
            weights_lo(len(SPLIT))
            acts_lo("gT", 2, 1, 2)
            for j in range(2):
                b = wait_full((GCN3B, j))
                v.tensor_tensor(x[:, hcols(j)], psum[b][0:N, :], x[:, hcols(j)], ALU.add).then_inc(out_ready, 1)

        @block.tensor
        def _(pe):
            t = nc.tensor
            owed = [False]

            def refill(key):
                b, n = FILL[key]
                if n > 1:
                    pe.wait_ge(drained[b], n - 1)
                return b

            def wait_drained(key):
                b, n = FILL[key]
                pe.wait_ge(drained[b], n)

            def bias(i):
                halves, cols = (1, F) if i == GCN3A else (2, HB)
                for j in range(halves):
                    b = refill((i, j))
                    terms = [(sel[:, i, :], b_hi), (sel[:, i, :], b_lo)]
                    if i == GCN2:
                        if j == 0:
                            wait_drained(("rowsum", 0))
                        terms = [(rs_hi[:, :], b_hi), (rs_hi[:, :], b_lo), (rs_lo[:, :], b_hi)]
                    for n, (lhs, rhs) in enumerate(terms):
                        ins = t.matmul(psum[b][0:N, 0:cols], lhs, rhs[:, j * HB:j * HB + cols], start=(n == 0), stop=False)
                        if owed[0]:
                            ins.then_inc(ring_free, 1)
                            owed[0] = False

            def product(i, slot, ready, first=0, last=True, begin=0, end=KC):
                for k in range(begin, end):
                    if k % HC == 0:
                        wait_drained((ready, k // HC))
                    g = 2 * (FIRST_UNIT[i] + first) + k
                    u = g // 2
                    final = last and k == KC - 1
                    if u in DIRECT_UNITS:
                        pe.wait_ge(raw_loaded[u % RAW], 16 * (u // RAW + 1))
                        for j in range(2):
                            ins = t.matmul(psum[FILL[i, j][0]][0:N, :], vT[:, k, :], raw[:, u % RAW, g % 2, hcols(j)],
                                           start=False, stop=False)
                        ins.then_inc(raw_used[u % RAW], 1)
                        continue
                    s = PLACE[g]
                    r = s % RING
                    wait_split(g)
                    hi, lo = a_hi[:, slot, k, :], a_lo[:, slot, k, :]
                    order = ([(j, n) for j in range(2) for n in range(3)] if final else
                             [(0, 0), (1, 0), (0, 1), (1, 1), (0, 2), (1, 2)])
                    for j, n in order:
                        lhs, rhs = ((hi, w_hi), (hi, w_lo), (lo, w_hi))[n]
                        b = FILL[i, j][0]
                        ins = t.matmul(psum[b][0:N, :], lhs, rhs[:, r, hcols(j)], start=False, stop=final and n == 2)
                        if final and n == 2:
                            ins.then_inc(full[b], 1)
                    if final:
                        owed[0] = True
                    else:
                        ins.then_inc(ring_free, 1)

            def wait_split(g):
                u, c = divmod(g, 2)
                pe.wait_ge(raw_used[u % RAW], 2 * (u // RAW) + c + 1)

            def transpose(name, tile, j):
                b = refill((name, j))
                for c in range(HC):
                    k = j * HC + c
                    ins = t.transpose(psum[b][:, c * N:(c + 1) * N], tile[:, k * P:(k + 1) * P], ident[:, :])
                ins.then_inc(full[b], 1)

            def aggregate(name, tile, AT, halves=2, k=HC):
                for j in range(halves):
                    b = refill((name, j))
                    for c in range(k):
                        kk = j * HC + c
                        ins = t.matmul(psum[b][:, c * N:(c + 1) * N], tile[:, kk * P:(kk + 1) * P], AT[:, :],
                                       start=True, stop=True)
                    ins.then_inc(full[b], 1)

            def transpose_result(name, i):
                for j in range(2):
                    wait_drained((i, j))
                    transpose(name, ev[:, i % 2, :], j)

            def compare_pairs(name, p):
                c0, c1 = PIECES[p]
                b = refill((name, p % 2))
                o = psum[b][0:N, 0:(c1 - c0) * N]
                t.matmul(o, ones[:, :], diag[:, c0:c1, :].rearrange("p c n -> p (c n)"), start=True, stop=False)
                t.matmul(o.rearrange("p (c n) -> p c n", n=N), ident_b[:, :],
                         tri_b[:, :].unsqueeze(1).to_broadcast([N, c1 - c0, N]), start=False, stop=True)\
                    .then_inc(full[b], 1)

            def pair_keys(name, p):
                c0, c1 = PIECES[p]
                b = refill((name, p % 2))
                for c in range(c0, c1):
                    ins = t.matmul(psum[b][0:N, (c - c0) * N:(c - c0 + 1) * N], oh_src[:, c, :], oh_key[:, c, :],
                                   start=True, stop=True)
                ins.then_inc(full[b], 1)

            pe.wait_ge(ident_ready, 1)
            for j in range(2):
                pe.wait_ge(normed, j + 1)
                transpose("h0T", h, j)
            pe.wait_ge(sel_ready, 1)
            pe.wait_ge(bias_lo, 1)
            bias(Q)
            product(Q, 0, "h0T")
            bias(K)
            product(K, 0, "h0T", end=2, last=False)
            transpose_result("qT", Q)
            product(K, 0, "h0T", begin=2, end=4, last=False)
            pe.wait_ge(diag_ready, 1)
            for p in (0, 1):
                compare_pairs("eqA", p)
            product(K, 0, "h0T", begin=4, end=6, last=False)
            for p in (2, 3):
                compare_pairs("eqB", p)
            product(K, 0, "h0T", begin=6)
            bias(V)
            product(V, 0, "h0T", end=2, last=False)
            transpose_result("kT", K)
            product(V, 0, "h0T", begin=2, end=4, last=False)
            pe.wait_ge(onehots_ready, 2 * EC)
            pe.wait_ge(keys_ready, EC)
            for p in (0, 1):
                pair_keys("keyA", p)
            product(V, 0, "h0T", begin=4, end=6, last=False)
            for p in (2, 3):
                pair_keys("keyB", p)
            product(V, 0, "h0T", begin=6)
            bias(Q2)
            product(Q2, 1, "qT", end=2, last=False)
            transpose_result("vT", V)
            product(Q2, 1, "qT", begin=2, end=4, last=False)
            b = refill(("counts", 0))
            for n, (lhs, rhs) in enumerate(((oh_src, oh_dst), (oh_dst, oh_src))):
                for c in range(EC):
                    ins = t.matmul(psum[b][0:N, n * N:(n + 1) * N], lhs[:, c, :], rhs[:, c, :], start=(c == 0),
                                   stop=(c == EC - 1))
            ins.then_inc(full[b], 1)
            product(Q2, 1, "qT", begin=4)
            bias(K2)
            product(K2, 2, "kT", end=1, last=False)
            wait_drained(("counts", 0))
            b = refill(("degrees", 0))
            for n in range(2):
                t.matmul(psum[b][0:N, n * N:(n + 1) * N], ones[:, :], C[:, n, :], start=True, stop=True)
                ins = t.matmul(psum[b][0:N, 2 * N + n:2 * N + n + 1], C[:, n, :], ones[:, 0:1], start=True, stop=True)
            ins.then_inc(full[b], 1)
            product(K2, 2, "kT", begin=1, end=2, last=False)
            transpose_result("q2T", Q2)
            product(K2, 2, "kT", begin=2)
            bias(V2)
            product(V2, 0, "vT", end=1, last=False)
            transpose_result("k2T", K2)
            product(V2, 0, "vT", begin=1, end=2, last=False)
            for e in range(2):
                wait_drained(("q2T", e))
                wait_drained(("k2T", e))
                for j in range(2):
                    b = refill((f"scores{e}", j))
                    for c in range(HC):
                        rows, kk = slice(DH * j, DH * j + DH), HC * e + c
                        ins = t.matmul(psum[b][0:N, c * N:(c + 1) * N], q2T[rows, kk, :], k2T[rows, kk, :],
                                       start=True, stop=True)
                    ins.then_inc(full[b], 1)
            product(V2, 0, "vT", begin=2)
            bias(O)
            for p in range(4):
                name = f"probsT{p // 2}"
                pe.wait_ge(probs_ready, p + 1)
                b = refill((name, p % 2))
                for c in range(4):
                    ins = t.transpose(psum[b][0:N, c * N:(c + 1) * N], S[:, 4 * p + c, :], ident[:, :])
                ins.then_inc(full[b], 1)
            for e in range(2):
                wait_drained((V2, e))
                for j in range(2):
                    wait_drained((f"probsT{e}", j))
                b = refill(("headsT", e))
                for c in range(HC):
                    for j in range(2):
                        head = 2 * (HC * e + c) + j
                        ins = t.matmul(psum[b][DH * j:DH * j + DH, c * N:(c + 1) * N],
                                       ev[:, V2 % 2, head * DH:(head + 1) * DH], PT[:, 8 * e + 4 * j + c, :],
                                       start=True, stop=True)
                ins.then_inc(full[b], 1)
            product(O, 1, "headsT")
            bias(SAGE0)
            for j in range(2):
                pe.wait_ge(normed, 2 + j + 1)
                transpose("h1T", h, j)
            pe.wait_ge(A1_ready, 1)
            aggregate("mean1T", h, A1T)
            product(SAGE0, 2, "h1T", last=False, end=4)
            pe.wait_ge(A23_ready, 1)
            b = refill(("rowsum", 0))
            t.matmul(psum[b][0:12, 0:N], bcol[:, :], A2T[:, :], start=True, stop=True).then_inc(full[b], 1)
            product(SAGE0, 2, "h1T", last=False, begin=4)
            product(SAGE0, 0, "mean1T", first=4)
            bias(SAGE1)
            transpose_result("hiddenT", SAGE0)
            aggregate("mean2T", ev[:, SAGE0 % 2, :], A1T)
            product(SAGE1, 1, "hiddenT", last=False)
            product(SAGE1, 2, "mean2T", first=4)
            bias(GCN2)
            pe.wait_ge(normed, 6)
            aggregate("h2T", h, A2T)
            product(GCN2, 0, "h2T")
            bias(GCN3A)
            pe.wait_ge(A23_ready, 2)
            pe.wait_ge(normed, 8)
            aggregate("h3T", h, A3T)
            b = FILL[GCN3A, 0][0]
            for k in range(KC):
                g = 2 * FIRST_UNIT[GCN3A] + k // 4
                if k % 4 == 0:
                    wait_drained(("h3T", k // HC))
                    wait_split(g)
                r, c = PLACE[g] % RING, slice((k % 4) * F, (k % 4 + 1) * F)
                for n, (lhs, rhs) in enumerate(((a_hi, w_hi), (a_hi, w_lo), (a_lo, w_hi))):
                    ins = t.matmul(psum[b][0:N, 0:F], lhs[:, 1, k, :], rhs[:, r, c], start=False,
                                   stop=(k == KC - 1 and n == 2))
            ins.then_inc(full[b], 1)
            bias(GCN3B)
            wait_drained((GCN3A, 0))
            aggregate("gT", ev[:, GCN3A % 2, :], A3T, 1, 2)
            wait_drained(("gT", 0))
            for k in range(2):
                wait_split(2 * FIRST_UNIT[GCN3B] + k)
            for j in range(2):
                b = FILL[GCN3B, j][0]
                for k in range(2):
                    r = PLACE[2 * FIRST_UNIT[GCN3B] + k] % RING
                    for n, (lhs, rhs) in enumerate(((a_hi, w_hi), (a_hi, w_lo), (a_lo, w_hi))):
                        ins = t.matmul(psum[b][0:N, :], lhs[:, 2, k, :], rhs[:, r, hcols(j)], start=False,
                                       stop=(k == 1 and n == 2))
                ins.then_inc(full[b], 1)


WEIGHTS = [("L0_gnn_wq", True), ("L0_gnn_wk", True), ("L0_gnn_wv", True), ("L0_gnn_wiq", True), ("L0_gnn_wik", True),
           ("L0_gnn_wiv", True), ("L0_gnn_wo", True), ("L1_gnn_W_self0", False), ("L1_gnn_W_neigh0", False),
           ("L1_gnn_W_self1", False), ("L1_gnn_W_neigh1", False), ("L2_gnn_W", True), ("L3_gnn_W1", False),
           ("L3_gnn_W2", False)]
BIASES = ["L0_gnn_bq", "L0_gnn_bk", "L0_gnn_bv", "L0_gnn_biq", "L0_gnn_bik", "L0_gnn_biv", "L0_gnn_bo", "L1_gnn_b0",
          "L1_gnn_b1", "L2_gnn_b", "L3_gnn_b1", "L3_gnn_b2"]


def kernel(**inputs):
    import numpy as np
    import concourse.bacc as bacc
    from concourse.bass_utils import run_bass_kernel_spmd

    units = []
    for name, transposed in WEIGHTS:
        w = np.asarray(inputs[name])
        w = w.T if transposed else w
        rows, cols = w.shape
        per = UNIT // cols
        w = w.reshape(rows // (per * P), per, P, cols).transpose(0, 2, 1, 3)
        units.append(w.reshape(-1, P, UNIT))
    biases = np.zeros((12, D), np.float32)
    for n, name in enumerate(BIASES):
        b = np.asarray(inputs[name])
        biases[n, :b.shape[0]] = b
    edges = np.stack([np.asarray(inputs[k]).reshape(EC, N).T for k in ("src", "dst", "edge_type_5")], axis=1)
    arrays = {
        "x": np.ascontiguousarray(inputs["x"]), "weights": np.concatenate(units), "biases": biases,
        "edges": np.ascontiguousarray(edges), "edge_w": np.asarray(inputs["L0_gnn_edge_type_weights"]).reshape(1, 4),
    }
    nc = bacc.Bacc("TRN2", target_bir_lowering=False, num_devices=1)
    args = [nc.dram_tensor(f"in_{k}", a.shape, mybir.dt.from_np(a.dtype), kind="ExternalInput").ap()
            for k, a in arrays.items()]
    args.append(nc.dram_tensor("out_x", (N, D), mybir.dt.float32, kind="ExternalOutput").ap())
    gnn_kernel(nc, *args)
    r = run_bass_kernel_spmd(nc, [{f"in_{k}": a for k, a in arrays.items()}], core_ids=[0])
    return r.results[0]["out_x"]
```

```python
import concourse.bass as bass
from concourse import mybir
from contextlib import ExitStack

N, D, F = 96, 1024, 256
P = 128
KC = D // P
H, DH = 16, 64
NE, EC = 1632, 17
HB = D // 2
HC = KC // 2
TW = HC * N
SR, BR = 44, 76
LN_EPS = 1e-5
SCALE = 1.0 / DH ** 0.5
NO_EDGE = -1.0e30
TRI = 32768.0
UNITS, UNIT = 50, 2 * D
RAW, RING = 5, 10

Q, K, V, Q2, K2, V2, O, SAGE0, SAGE1, GCN2, GCN3A, GCN3B = range(12)
FIRST_UNIT = {Q: 0, K: 4, V: 8, Q2: 12, K2: 16, V2: 20, O: 24, SAGE0: 28, SAGE1: 36, GCN2: 44, GCN3A: 48, GCN3B: 49}

CHUNKS = 2 * UNITS
BY_DVE = 1
BEFORE = {i: 2 * u for i, u in FIRST_UNIT.items()}

EVENTS = [("h0T", 2), ("eqA", 2), ("eqB", 2), ("qT", 2), ("voids", 1), ("kT", 2), ("keyA", 2), ("keyB", 2),
          ("counts", 1), ("vT", 2), ("degrees", 1), ("q2T", 2), ("k2T", 2), ("scores0", 2), ("scores1", 2), ("probsT0", 2), ("probsT1", 2),
          ("headsT", 2), ("h1T", 2), ("mean1T", 2), ("rowsum", 1), ("hiddenT", 2), ("mean2T", 2), ("h2T", 2),
          ("h3T", 2), ("gT", 1)]


def bank_fills():
    count, out = [0] * 8, {}
    for t, (name, halves) in enumerate(EVENTS):
        for j in range(halves):
            b = 4 + 2 * (t % 2) + j
            count[b] += 1
            out[name, j] = (b, count[b])
    return out


FILL = bank_fills()
for _i in range(12):
    for _j in range(2):
        FILL[_i, _j] = (2 * (_i % 2) + _j, _i // 2 + 1)

WARM = {"h0T": 10, "eqA": 3, "h1T": 14, "hiddenT": 2, "h2T": 14, "h3T": 14}

PIECES = [(0, 5), (5, 9), (9, 13), (13, 17)]
ACT_HI = ["h0T", "qT", "kT", "vT", "headsT", "h1T", "mean1T", "hiddenT", "mean2T", "h2T", "h3T", "gT"]
HI_COUNT = {}
for _name in ACT_HI:
    for _j in range(1 if _name == "gT" else 2):
        HI_COUNT[_name, _j] = len(HI_COUNT) + 1


def gnn_kernel(nc, x_in, weights, biases, edges, edge_w, out):
    f32, f32r, bf16, i32 = mybir.dt.float32, mybir.dt.float32r, mybir.dt.bfloat16, mybir.dt.int32
    ALU, ACT, AX = mybir.AluOpType, mybir.ActivationFunctionType, mybir.AxisListType
    ctx = ExitStack()
    with ctx:
        def sb(name, shape, dt=f32):
            return ctx.enter_context(nc.sbuf_tensor(name, shape, dt))

        def sem(name):
            return ctx.enter_context(nc.semaphore(name))

        raw = sb("raw", [P, RAW, 2, D])
        w_hi = sb("w_hi", [P, RING, D], f32r)
        w_lo = sb("w_lo", [P, RING, D], f32r)
        x = sb("x", [N, D])
        h = sb("h", [N, D])
        ev = sb("ev", [N, 2, D])
        a_hi = sb("a_hi", [P, 3, KC, N], f32r)
        a_lo = sb("a_lo", [P, 3, KC, N], f32r)
        q2T = sb("q2T", [P, KC, N])
        k2T = sb("k2T", [P, KC, N])
        S = sb("S", [N, EC, N])
        PT = sb("PT", [N, EC, N])
        onehot = PT[:, :, :].rearrange("p c n -> p (c n)").bitcast(bf16).rearrange("p (k c n) -> p k c n", k=2, c=EC)
        oh_src, oh_dst = onehot[:, 0], onehot[:, 1]
        diag = S
        oh_key = sb("oh_key", [N, EC, N], bf16)
        same = oh_key
        b_parts = sb("b_parts", [BR, D], f32r)
        b_raw = ev[0:BR, 1, :]
        sel = sb("sel", [SR, 12, N], f32r)
        sel_f = S[0:SR, 0:12, :]
        rs = sb("rs", [BR, N], f32r)
        warm = sb("warm", [P, HB], bf16)
        ident = sb("ident", [N, N])
        ident_b = sb("ident_b", [N, N], bf16)
        ones = sb("ones", [N, N])
        ones_b = sb("ones_b", [N, 1], bf16)
        tri_b = sb("tri_b", [N, N], bf16)
        iota_i = sb("iota_i", [N, N], i32)
        iota_f = sb("iota_f", [N, N])
        bcol = sb("bcol", [N, 12])
        edges_i = sb("edges_i", [N, 3, EC], i32)
        edges_f = sb("edges_f", [N, 3, EC])
        src, dst, typ = (edges_f[:, n, :] for n in range(3))
        pair = sb("pair", [N, EC])
        key_i = sb("key_i", [N, EC], i32)
        key = sb("key", [N, EC])
        live = sb("live", [N, EC])
        kmax = sb("kmax", [N, 4, N])
        kind_i = sb("kind_i", [N, 2, N], i32)
        kind = sb("kind", [N, N])
        mterm = sb("mterm", [N, 3, N])
        mask = sb("mask", [N, N])
        ew = sb("ew", [N, 4])
        ews = sb("ews", [N, 4, 4])
        C = sb("C", [N, 2, N])
        deg = sb("deg", [N, 2 * N + 2])
        dis = sb("dis", [N, 2, 2 * N + 2])
        mdeg = sb("mdeg", [N, 2, N])
        A1T = sb("A1T", [N, N])
        A2T = sb("A2T", [N, N])
        A3T = sb("A3T", [N, N])
        atmp = sb("atmp", [N, 4, N])
        stats = sb("stats", [N, 2, 6])
        mv = sb("mv", [N, 2])
        std = sb("std", [N, 2])
        eps = sb("eps", [N, 1])
        early = sb("early", [N, 1])
        scaled_m = sb("scaled_m", [N, 2, N])
        nmax = sb("nmax", [N, H])
        rsum = sb("rsum", [N, 2, H])
        psum = [ctx.enter_context(nc.psum_tensor(f"bank{b}", [P, HB], f32)) for b in range(8)]

        x_loaded = [sem(f"x_loaded{j}") for j in range(2)]
        edges_loaded, biases_loaded, ew_loaded = sem("edges_loaded"), sem("biases_loaded"), sem("ew_loaded")
        raw_loaded = [sem(f"raw_loaded{r}") for r in range(RAW)]
        raw_used = [sem(f"raw_used{r}") for r in range(RAW)]
        hi_ready = sem("hi_ready")
        first_hi = sem("first_hi")
        ring_free = sem("ring_free")
        full = [sem(f"full{b}") for b in range(8)]
        drained = [sem(f"drained{b}") for b in range(8)]
        act_hi = sem("act_hi")
        centered = sem("centered")
        scaled = sem("scaled")
        eps_ready, var_ready, std_ready = sem("eps_ready"), sem("var_ready"), sem("std_ready")
        cleared, bias_hi, bias_lo = sem("cleared"), sem("bias_hi"), sem("bias_lo")
        warm_ready, sel_f_ready, sel_ready, ident_ready = sem("warm_ready"), sem("sel_f_ready"), sem("sel_ready"), sem("ident_ready")
        diag_ready, tri_ready, live_ready = sem("diag_ready"), sem("tri_ready"), sem("live_ready")
        onehots_ready, keys_ready = sem("onehots_ready"), sem("keys_ready")
        kind_ready, ew_ready, mask_ready = sem("kind_ready"), sem("ew_ready"), sem("mask_ready")
        mdeg_ready, sdeg_ready, dis_ready = sem("mdeg_ready"), sem("sdeg_ready"), sem("dis_ready")
        A1_ready, A23_ready = sem("A1_ready"), sem("A23_ready")
        max_ready, exp_ready, inverse_ready = sem("max_ready"), sem("exp_ready"), sem("inverse_ready")
        probs_ready = sem("probs_ready")
        pool_step, dve_step, act_step = sem("pool_step"), sem("dve_step"), sem("act_step")
        out_ready, stored = sem("out_ready"), sem("stored")

        def tcols(j):
            return slice(j * HC, (j + 1) * HC)

        def hcols(j):
            return slice(j * HB, (j + 1) * HB)

        def tview(b, rows=P, k=HC):
            return psum[b][0:rows, 0:k * N].rearrange("p (c n) -> p c n", n=N)

        block = ctx.enter_context(nc.Block())

        @block.sync
        def _(sp):
            for j in range(2):
                sp.dma_start(x[:, hcols(j)], x_in[:, hcols(j)]).then_inc(x_loaded[j], 16)

            def load(u, r):
                sp.dma_start(raw[:, r, :, :].rearrange("p c n -> p (c n)"), weights[u]).then_inc(raw_loaded[r], 16)

            load(0, 0)
            sp.dma_start(edges_i[:, :, :], edges).then_inc(edges_loaded, 16)
            sp.wait_ge(cleared, 1)
            for p in (0, 32, 64):
                sp.dma_start(b_raw[p:p + 12, :], biases).then_inc(biases_loaded, 16)
            sp.dma_start(ew[:, :], edge_w.to_broadcast([N, 4])).then_inc(ew_loaded, 16)
            for r in range(1, RAW):
                load(r, r)
            with sp.Fori(1, UNITS // RAW) as turn:
                for r in range(RAW):
                    sp.wait_ge(raw_used[r], turn * 2)
                    load(turn * RAW + r, r)
            for j in range(2):
                sp.wait_ge(out_ready, j + 1)
                sp.dma_start(out[:, hcols(j)], x[:, hcols(j)]).then_inc(stored, 16)
            sp.wait_ge(stored, 32)

        @block.gpsimd
        def _(pool):
            steps = [0]

            def step(ins):
                steps[0] += 1
                ins.then_inc(pool_step, 1)
                pool.wait_ge(pool_step, steps[0])

            g = nc.gpsimd
            step(g.memset(ident[:, :], 0.0))
            g.affine_select(out=ident[:, :], in_=ident[:, :], compare_op=ALU.not_equal, fill=1.0, base=0,
                            pattern=[[-1, N]], channel_multiplier=1).then_inc(ident_ready, 1)
            step(g.memset(sel_f, 0.0))
            for base in (0, 32):
                ins = g.affine_select(out=sel_f, in_=sel_f, compare_op=ALU.not_equal, fill=1.0, base=base,
                                      pattern=[[1, 12], [0, N]], channel_multiplier=-1)
                if base == 0:
                    step(ins)
                else:
                    ins.then_inc(sel_f_ready, 1)
            pool.wait_ge(bias_hi, 1)
            pool.wait_ge(sel_f_ready, 1)
            g.tensor_tensor(b_parts[32:SR, :], b_raw[32:SR, :], b_parts[32:SR, :].bitcast(f32), ALU.subtract)\
                .then_inc(bias_lo, 1)
            pool.wait_ge(bias_lo, 1)
            step(g.iota(iota_i[:, :], [[1, N]], base=0, channel_multiplier=0))
            step(g.tensor_copy(iota_f[:, :], iota_i[:, :]))
            step(g.iota(key_i[:, :], [[8, EC]], base=1, channel_multiplier=0))
            step(g.tensor_copy(key[:, :], key_i[:, :]))
            pool.wait_ge(edges_loaded, 16)
            step(g.tensor_copy(edges_f[:, :, :], edges_i[:, :, :]))
            step(g.tensor_scalar(pair[:, :], src, float(N), 0.0, ALU.mult, ALU.add))
            step(g.tensor_tensor(pair[:, :], pair[:, :], dst, ALU.add))
            step(g.tensor_tensor(key[:, :], key[:, :], typ, ALU.add))
            pool.wait_ge(sel_ready, 1)
            pool.wait_ge(ident_ready, 1)
            g.tensor_tensor(diag[:, :, :], ident[:, :].unsqueeze(1).to_broadcast([N, EC, N]),
                            pair[:, :].unsqueeze(2).to_broadcast([N, EC, N]), ALU.mult).then_inc(diag_ready, 1)
            step(g.tensor_copy(ident_b[:, :], ident[:, :]))
            step(g.memset(ones[:, :], 1.0))
            step(g.tensor_copy(ones_b[:, :], ones[:, 0:1]))
            step(g.affine_select(out=tri_b[:, :], in_=ones[:, :], compare_op=ALU.is_ge, fill=0.0, base=0,
                                 pattern=[[1, N]], channel_multiplier=-1))
            g.tensor_scalar(tri_b[:, :], tri_b[:, :], TRI, 1.0, ALU.mult, ALU.mult).then_inc(tri_ready, 1)
            step(g.memset(bcol[:, :], 0.0))
            step(g.memset(bcol[:, GCN2:GCN2 + 1], 1.0))
            for c in range(EC):
                g.tensor_scalar(oh_src[:, c, :], iota_f[:, :], src[:, c:c + 1], None, ALU.is_equal)\
                    .then_inc(onehots_ready, 1)
                g.tensor_scalar(oh_dst[:, c, :], iota_f[:, :], dst[:, c:c + 1], None, ALU.is_equal)\
                    .then_inc(onehots_ready, 1)
            pool.wait_ge(onehots_ready, 2 * EC)
            pool.wait_ge(live_ready, 1)
            g.tensor_tensor(oh_key[:, :, :], oh_dst, live[:, :].unsqueeze(2).to_broadcast([N, EC, N]), ALU.mult)\
                .then_inc(keys_ready, 1)
            pool.wait_ge(kind_ready, 1)
            pool.wait_ge(ew_ready, 1)
            none, off, on = (mterm[:, n, :] for n in range(3))
            w = ews[:, 3, :]
            step(g.tensor_scalar(none, kind[:, :], 0.0, None, ALU.is_equal))
            step(g.tensor_tensor(on, none, ident[:, :], ALU.mult))
            step(g.tensor_tensor(off, none, on, ALU.subtract))
            step(g.tensor_scalar(off, off, NO_EDGE, 0.0, ALU.mult, ALU.add))
            step(g.tensor_scalar(on, on, w[:, 3:4], 0.0, ALU.mult, ALU.add))
            step(g.tensor_tensor(mask[:, :], off, on, ALU.add))
            for k, m in ((1, 3), (2, 0), (3, 1), (4, 2), (5, 3)):
                step(g.tensor_scalar(on, kind[:, :], float(k), w[:, m:m + 1], ALU.is_equal, ALU.mult))
                ins = g.tensor_tensor(mask[:, :], mask[:, :], on, ALU.add)
                if k < 5:
                    step(ins)
                else:
                    ins.then_inc(mask_ready, 1)
            pool.wait_ge(mdeg_ready, 1)
            g.tensor_tensor(A1T[:, :], C[:, 0, :], mdeg[:, 1, :], ALU.mult).then_inc(A1_ready, 1)
            for p in range(4):
                heads = slice(4 * p, 4 * p + 4)
                pool.wait_ge(inverse_ready, p + 1)
                g.tensor_tensor(S[:, heads, :], S[:, heads, :],
                                rsum[:, 1, heads].unsqueeze(2).to_broadcast([N, 4, N]), ALU.mult)\
                    .then_inc(probs_ready, 1)
            pool.wait_ge(dis_ready, 1)
            for k, (cc, AT) in enumerate(((1, A2T), (0, A3T))):
                by = 1 - k
                step(g.tensor_tensor(atmp[:, 2 * k, :], C[:, cc, :], ident[:, :], ALU.add))
                step(g.tensor_tensor(atmp[:, 2 * k + 1, :], atmp[:, 2 * k, :], dis[:, 1, by * N:(by + 1) * N], ALU.mult))
                g.tensor_scalar(AT[:, :], atmp[:, 2 * k + 1, :], dis[:, 1, 2 * N + by:2 * N + by + 1], 0.0,
                                ALU.mult, ALU.add).then_inc(A23_ready, 1)

        @block.scalar
        def _(act):
            a = nc.scalar
            steps, done = [0], [BY_DVE]

            def step(ins):
                steps[0] += 1
                ins.then_inc(act_step, 1)
                act.wait_ge(act_step, steps[0])

            def weights_hi(upto):
                while done[0] < min(upto, CHUNKS):
                    s = done[0]
                    u, c = divmod(s, 2)
                    if c == 0 or s == BY_DVE:
                        act.wait_ge(raw_loaded[u % RAW], 16 * (u // RAW + 1))
                    if s >= RING:
                        act.wait_ge(ring_free, s - RING + 1)
                    a.activation(w_hi[:, s % RING, :], raw[:, u % RAW, c, :], ACT.Copy).then_inc(hi_ready, 1)
                    done[0] += 1

            def wait_full(key):
                b, n = FILL[key]
                act.wait_ge(full[b], n)
                return b

            def copy_out(i, halves=(0, 1), func=ACT.Copy, cols=HB):
                for j in halves:
                    b = wait_full((i, j))
                    a.activation(ev[:, i % 2, j * HB:j * HB + cols], psum[b][0:N, 0:cols], func)\
                        .then_inc(drained[b], 1)

            def acts_hi(name, slot, halves=(0, 1), k=HC):
                for j in halves:
                    b = wait_full((name, j))
                    a.activation(a_hi[:, slot, j * HC:j * HC + k, :], tview(b, k=k), ACT.Copy).then_inc(act_hi, 1)

            def transposed_out(name, j, tile, scale=1.0):
                b = wait_full((name, j))
                a.activation(tile[:, tcols(j), :], tview(b), ACT.Copy, scale=scale).then_inc(drained[b], 1)

            def norm(layer):
                act.wait_ge(var_ready, layer + 1)
                a.activation(std[:, 0:1], mv[:, 1:2], ACT.Sqrt, bias=eps[:, :]).then_inc(std_ready, 1)

            act.wait_ge(eps_ready, 1)
            a.activation(early[:, :], eps[:, :], ACT.Sqrt)
            norm(0)
            act.wait_ge(sel_f_ready, 1)
            a.activation(sel[:, :, :], sel_f, ACT.Copy).then_inc(sel_ready, 1)
            acts_hi("h0T", 0, (0,))
            weights_hi(2)
            acts_hi("h0T", 0, (1,))
            weights_hi(3)
            act.wait_ge(biases_loaded, 48)
            a.activation(b_parts[:, :], b_raw, ACT.Copy).then_inc(bias_hi, 1)
            weights_hi(BEFORE[K] + 2)
            copy_out(Q)
            weights_hi(BEFORE[V] + 1)
            acts_hi("qT", 1)
            weights_hi(BEFORE[V] + 4)
            copy_out(K)
            weights_hi(BEFORE[Q2] + 3)
            acts_hi("kT", 2)
            weights_hi(BEFORE[Q2] + 5)
            copy_out(V)
            weights_hi(BEFORE[Q2] + 7)
            act.wait_ge(ew_loaded, 16)
            step(a.activation(ews[:, 0, :], ew[:, :], ACT.Abs))
            step(a.activation(ews[:, 1, :], ews[:, 0, :], ACT.Exp, scale=-1.0))
            step(a.activation(ews[:, 2, :], ews[:, 1, :], ACT.Ln, bias=1.0))
            weights_hi(BEFORE[K2] + 4)
            acts_hi("vT", 0)
            weights_hi(BEFORE[K2] + 5)
            copy_out(Q2)
            weights_hi(BEFORE[V2] + 4)
            transposed_out("q2T", 0, q2T, SCALE)
            transposed_out("q2T", 1, q2T, SCALE)
            weights_hi(BEFORE[V2] + 7)
            copy_out(K2)
            transposed_out("k2T", 0, k2T)
            weights_hi(BEFORE[V2] + 7)
            for p in range(4):
                b, _ = FILL[f"scores{p // 2}", p % 2]
                act.wait_ge(max_ready, p + 1)
                for c in range(4):
                    hh = 4 * p + c
                    a.activation(S[:, hh, :], psum[b][0:N, c * N:(c + 1) * N], ACT.Exp, bias=nmax[:, hh:hh + 1],
                                 accum_out=rsum[:, 0, hh:hh + 1]).then_inc(exp_ready if c < 3 else drained[b], 1)
                weights_hi(BEFORE[V2] + 8 + 2 * p)
            copy_out(V2, (0,))
            for p in (0, 2):
                b = wait_full((f"probsT{p // 2}", p % 2))
                a.activation(PT[:, 4 * p:4 * p + 4, :], tview(b, N), ACT.Copy).then_inc(drained[b], 1)
            acts_hi("headsT", 1)
            weights_hi(BEFORE[SAGE0] + 3)
            norm(1)
            weights_hi(BEFORE[SAGE0] + 4)
            acts_hi("h1T", 2)
            acts_hi("mean1T", 0)
            b, n = FILL["degrees", 0]
            act.wait_ge(drained[b], n)
            a.activation(dis[:, 0, :], deg[:, :], ACT.Sqrt).then_inc(sdeg_ready, 1)
            weights_hi(BEFORE[SAGE1] + 3)
            copy_out(SAGE0, (0,), ACT.Relu)
            weights_hi(BEFORE[SAGE1] + 3)
            acts_hi("hiddenT", 1)
            acts_hi("mean2T", 2)
            weights_hi(BEFORE[GCN2] + 3)
            norm(2)
            weights_hi(BEFORE[GCN2] + 4)
            acts_hi("h2T", 0)
            weights_hi(BEFORE[GCN3A] + 3)
            norm(3)
            acts_hi("h3T", 1)
            weights_hi(CHUNKS)
            copy_out(GCN3A, (0,), ACT.Relu, F)
            acts_hi("gT", 2, (0,), 2)

        @block.vector
        def _(dve):
            v = nc.vector
            steps, done = [0], [0]

            def step(ins):
                steps[0] += 1
                ins.then_inc(dve_step, 1)
                dve.wait_ge(dve_step, steps[0])

            def weights_lo(upto):
                while done[0] < min(upto, CHUNKS):
                    s = done[0]
                    u, c = divmod(s, 2)
                    if s < BY_DVE:
                        dve.wait_ge(first_hi, s + 1)
                    else:
                        dve.wait_ge(hi_ready, s - BY_DVE + 1)
                    v.tensor_tensor(w_lo[:, s % RING, :], raw[:, u % RAW, c, :], w_hi[:, s % RING, :].bitcast(f32),
                                    ALU.subtract).then_inc(raw_used[u % RAW], 1)
                    done[0] += 1

            def wait_full(key):
                b, n = FILL[key]
                dve.wait_ge(full[b], n)
                return b

            def copy_out(i, j):
                b = wait_full((i, j))
                v.tensor_copy(ev[:, i % 2, hcols(j)], psum[b][0:N, :]).then_inc(drained[b], 1)

            def acts_lo(name, slot, halves=(0, 1), k=HC):
                for j in halves:
                    b, _ = FILL[name, j]
                    dve.wait_ge(act_hi, HI_COUNT[name, j])
                    v.tensor_tensor(a_lo[:, slot, j * HC:j * HC + k, :], tview(b, k=k),
                                    a_hi[:, slot, j * HC:j * HC + k, :].bitcast(f32), ALU.subtract)\
                        .then_inc(drained[b], 1)

            def transposed_out(name, j, tile):
                b = wait_full((name, j))
                v.tensor_copy(tile[:, tcols(j), :], tview(b)).then_inc(drained[b], 1)

            def residual(i):
                for j in range(2):
                    b = wait_full((i, j))
                    v.tensor_tensor(x[:, hcols(j)], psum[b][0:N, :], x[:, hcols(j)], ALU.add).then_inc(drained[b], 1)
                    dve.wait_ge(drained[b], FILL[i, j][1])
                    ins = v.bn_stats(stats[:, j, :], x[:, hcols(j)])
                    if j == 1:
                        step(ins)
                    else:
                        ins.then_inc(dve_step, 1)
                        steps[0] += 1

            def norm(layer, matrices):
                v.bn_aggr(mv[:, :], stats[:, :, :].rearrange("p a b -> p (a b)")).then_inc(var_ready, 1)
                dve.wait_ge(var_ready, layer + 1)
                v.tensor_scalar(h[:, hcols(0)], x[:, hcols(0)], mv[:, 0:1], 0.0, ALU.subtract, ALU.max)\
                    .then_inc(centered, 1)
                dve.wait_ge(std_ready, layer + 1)
                step(v.reciprocal(std[:, 1:2], std[:, 0:1]))
                for n, M in enumerate(matrices):
                    v.tensor_scalar(scaled_m[:, n, :], M[:, :], std[:, 1:2], None, ALU.mult).then_inc(scaled, 1)
                    if n == 0:
                        v.tensor_scalar(h[:, hcols(1)], x[:, hcols(1)], mv[:, 0:1], 0.0, ALU.subtract, ALU.max)\
                            .then_inc(centered, 1)

            v.memset(eps[:, :], LN_EPS).then_inc(eps_ready, 1)
            v.memset(warm[:, :], 0.0).then_inc(warm_ready, 1)
            v.memset(b_raw, 0.0).then_inc(cleared, 1)
            step(v.memset(rs[:, :].bitcast(f32), 0.0))
            for j in range(2):
                dve.wait_ge(x_loaded[j], 16)
                step(v.bn_stats(stats[:, j, :], x[:, hcols(j)]))
            dve.wait_ge(ident_ready, 1)
            norm(0, (ident,))
            dve.wait_ge(raw_loaded[0], 16)
            for s in range(BY_DVE):
                v.tensor_copy(w_hi[:, s, :], raw[:, 0, s, :]).then_inc(first_hi, 1)
            weights_lo(1)
            acts_lo("h0T", 0, (0,))
            weights_lo(2)
            acts_lo("h0T", 0, (1,))
            weights_lo(BEFORE[K] + 4)

            def mark_same(name, p):
                c0, c1 = PIECES[p]
                b = wait_full((name, p % 2))
                v.tensor_tensor(same[:, c0:c1, :], tview(b, N, c1 - c0),
                                pair[:, c0:c1].unsqueeze(2).to_broadcast([N, c1 - c0, N]), ALU.is_equal)\
                    .then_inc(drained[b], 1)

            dve.wait_ge(diag_ready, 1)
            mark_same("eqA", 0)
            mark_same("eqA", 1)
            weights_lo(BEFORE[K] + 6)
            mark_same("eqB", 2)
            mark_same("eqB", 3)
            weights_lo(BEFORE[V] + 1)
            acts_lo("qT", 1)
            weights_lo(BEFORE[V] + 3)
            b = wait_full(("voids", 0))
            v.tensor_scalar(live[:, :], psum[b][0:N, 0:EC], 0.0, None, ALU.is_equal).then_inc(drained[b], 1)
            dve.wait_ge(drained[b], FILL["voids", 0][1])
            v.tensor_tensor(live[:, :], live[:, :], key[:, :], ALU.mult).then_inc(live_ready, 1)
            weights_lo(BEFORE[Q2] + 2)
            acts_lo("kT", 2)

            def last_keys(name, p):
                c0, c1 = PIECES[p]
                b = wait_full((name, p % 2))
                v.tensor_reduce(out=kmax[:, p, :], in_=tview(b, N, c1 - c0).rearrange("p c d -> p d c"), axis=AX.X,
                                op=ALU.max).then_inc(drained[b], 1)

            weights_lo(BEFORE[Q2] + 4)
            last_keys("keyA", 0)
            last_keys("keyA", 1)
            weights_lo(BEFORE[Q2] + 5)
            last_keys("keyB", 2)
            last_keys("keyB", 3)
            for p in range(4):
                b, n = FILL[("keyA", "keyB")[p // 2], p % 2]
                dve.wait_ge(drained[b], n)
            step(v.tensor_tensor(kmax[:, 0:2, :], kmax[:, 0:2, :], kmax[:, 2:4, :], ALU.max))
            step(v.tensor_tensor(kmax[:, 0, :], kmax[:, 0, :], kmax[:, 1, :], ALU.max))
            step(v.tensor_copy(kind_i[:, 0, :], kmax[:, 0, :]))
            step(v.tensor_scalar(kind_i[:, 1, :], kind_i[:, 0, :], 7, None, ALU.bitwise_and))
            v.tensor_copy(kind[:, :], kind_i[:, 1, :]).then_inc(kind_ready, 1)
            dve.wait_ge(act_step, 3)
            v.scalar_tensor_tensor(ews[:, 3, :], ew[:, :], 0.0, ews[:, 2, :], ALU.max, ALU.add).then_inc(ew_ready, 1)
            weights_lo(BEFORE[Q2] + 7)
            b = wait_full(("counts", 0))
            v.tensor_copy(C[:, :, :], tview(b, N, 2)).then_inc(drained[b], 1)
            weights_lo(BEFORE[K2] + 2)
            acts_lo("vT", 0)
            weights_lo(BEFORE[K2] + 5)
            b = wait_full(("degrees", 0))
            step(v.tensor_scalar(mdeg[:, 0, :], psum[b][0:N, 0:N], 1.0, None, ALU.max))
            v.reciprocal(mdeg[:, 1, :], mdeg[:, 0, :]).then_inc(mdeg_ready, 1)
            v.tensor_scalar(deg[:, :], psum[b][0:N, 0:2 * N + 2], 1.0, None, ALU.add).then_inc(drained[b], 1)
            weights_lo(BEFORE[V2] + 5)
            transposed_out("k2T", 1, k2T)
            weights_lo(BEFORE[V2] + 6)
            def sums_inverted(p):
                heads = slice(4 * p, 4 * p + 4)
                dve.wait_ge(exp_ready, 3 * p + 3)
                b, n = FILL[f"scores{p // 2}", p % 2]
                dve.wait_ge(drained[b], n)
                v.reciprocal(rsum[:, 1, heads], rsum[:, 0, heads]).then_inc(inverse_ready, 1)

            for p in range(4):
                b = wait_full((f"scores{p // 2}", p % 2))
                v.tensor_reduce(out=nmax[:, 4 * p:4 * p + 4], in_=tview(b, N), axis=AX.X, op=ALU.max, negate=True)\
                    .then_inc(max_ready, 1)
                if p >= 1:
                    weights_lo(BEFORE[V2] + 6 + p)
                    sums_inverted(p - 1)
            weights_lo(BEFORE[V2] + 10)
            sums_inverted(3)
            weights_lo(BEFORE[O] + 3)
            copy_out(V2, 1)
            for p in (1, 3):
                b = wait_full((f"probsT{p // 2}", p % 2))
                v.tensor_copy(PT[:, 4 * p:4 * p + 4, :], tview(b, N)).then_inc(drained[b], 1)
            acts_lo("headsT", 1)
            weights_lo(BEFORE[SAGE0] + 2)
            residual(O)
            dve.wait_ge(A1_ready, 1)
            norm(1, (ident, A1T))
            weights_lo(BEFORE[SAGE0] + 4)
            acts_lo("h1T", 2)
            acts_lo("mean1T", 0)
            dve.wait_ge(sdeg_ready, 1)
            v.reciprocal(dis[:, 1, :], dis[:, 0, :]).then_inc(dis_ready, 1)
            weights_lo(BEFORE[SAGE0] + 8)
            b = wait_full(("rowsum", 0))
            for p in (0, 32):
                step(v.tensor_copy(rs[p:p + 12, :], psum[b][0:12, 0:N]))
            v.tensor_tensor(rs[64:76, :], psum[b][0:12, 0:N], rs[0:12, :].bitcast(f32), ALU.subtract)\
                .then_inc(drained[b], 1)
            weights_lo(BEFORE[SAGE1] + 2)
            b = wait_full((SAGE0, 1))
            v.tensor_scalar(ev[:, SAGE0 % 2, hcols(1)], psum[b][0:N, :], 0.0, None, ALU.max).then_inc(drained[b], 1)
            weights_lo(BEFORE[SAGE1] + 3)
            acts_lo("hiddenT", 1)
            acts_lo("mean2T", 2)
            weights_lo(BEFORE[GCN2] + 2)
            residual(SAGE1)
            dve.wait_ge(A23_ready, 2)
            norm(2, (A2T,))
            weights_lo(BEFORE[GCN2] + 4)
            acts_lo("h2T", 0)
            weights_lo(BEFORE[GCN3A] + 2)
            residual(GCN2)
            norm(3, (A3T,))
            weights_lo(BEFORE[GCN3A] + 3)
            acts_lo("h3T", 1)
            weights_lo(CHUNKS)
            acts_lo("gT", 2, (0,), 2)
            for j in range(2):
                b = wait_full((GCN3B, j))
                v.tensor_tensor(x[:, hcols(j)], psum[b][0:N, :], x[:, hcols(j)], ALU.add).then_inc(out_ready, 1)

        @block.tensor
        def _(pe):
            t = nc.tensor
            owed = [False]

            def refill(key):
                b, n = FILL[key]
                if n > 1:
                    pe.wait_ge(drained[b], n - 1)
                return b

            def wait_drained(key):
                b, n = FILL[key]
                pe.wait_ge(drained[b], n)

            def bias(i, opens=True):
                halves, cols = (1, F) if i == GCN3A else (2, HB)
                for j in range(halves):
                    b = refill((i, j))
                    if i == GCN2:
                        if j == 0:
                            wait_drained(("rowsum", 0))
                        lhs, rows = rs[:, :], BR
                    else:
                        lhs, rows = sel[:, i, :], SR
                    ins = t.matmul(psum[b][0:N, 0:cols], lhs, b_parts[0:rows, j * HB:j * HB + cols], start=opens,
                                   stop=False)
                    if owed[0]:
                        ins.then_inc(ring_free, 1)
                        owed[0] = False

            def keep_warm(name, count=None):
                b = refill((name, 0))
                for _ in range(count or WARM[name]):
                    t.matmul(psum[b][0:N, :], warm[:, 0:N], warm[:, :], start=True, stop=True)

            def wait_high(key):
                pe.wait_ge(act_hi, HI_COUNT[key])

            def product(i, slot, ready, first=0, last=True, begin=0, end=KC, opens=False):
                g0 = 2 * (FIRST_UNIT[i] + first)
                banks = [FILL[i, j][0] for j in range(2)]

                def term(k, n, j, start=False, stop=False):
                    lhs, rhs = ((a_hi, w_hi), (a_hi, w_lo), (a_lo, w_hi))[n]
                    return t.matmul(psum[banks[j]][0:N, :], lhs[:, slot, k, :], rhs[:, (g0 + k) % RING, hcols(j)],
                                    start=start, stop=stop)

                k = begin
                while k < end:
                    if k % HC == 0 and k > 0:
                        wait_drained((ready, k // HC))
                    if k == 0:
                        wait_high((ready, 0))
                        for kk in (0, 1):
                            wait_split(g0 + kk)
                            for n in (0, 1):
                                for j in range(2):
                                    term(kk, n, j, start=opens and kk == n == 0)
                        wait_drained((ready, 0))
                        for kk in (0, 1):
                            for j in range(2):
                                ins = term(kk, 2, j)
                            ins.then_inc(ring_free, 1)
                        k += 2
                    elif last and k == KC - 2:
                        for kk in (k, k + 1):
                            wait_split(g0 + kk)
                        for j in range(2):
                            for kk in (k, k + 1):
                                for n in range(3):
                                    ins = term(kk, n, j, stop=(kk == KC - 1 and n == 2))
                                if kk == k and j == 1:
                                    ins.then_inc(ring_free, 1)
                            ins.then_inc(full[banks[j]], 1)
                        owed[0] = True
                        k += 2
                    else:
                        wait_split(g0 + k)
                        for n in range(3):
                            for j in range(2):
                                ins = term(k, n, j)
                        ins.then_inc(ring_free, 1)
                        k += 1

            def wait_split(g):
                u, c = divmod(g, 2)
                pe.wait_ge(raw_used[u % RAW], 2 * (u // RAW) + c + 1)

            def transpose(name, tile, j):
                b = refill((name, j))
                for c in range(HC):
                    k = j * HC + c
                    ins = t.transpose(psum[b][:, c * N:(c + 1) * N], tile[:, k * P:(k + 1) * P], ident[:, :])
                ins.then_inc(full[b], 1)

            def aggregate(name, tile, AT, halves=2, k=HC, layer=None):
                for j in range(halves):
                    if layer is not None:
                        pe.wait_ge(centered, 2 * layer + j + 1)
                    b = refill((name, j))
                    for c in range(k):
                        kk = j * HC + c
                        ins = t.matmul(psum[b][:, c * N:(c + 1) * N], tile[:, kk * P:(kk + 1) * P], AT, start=True,
                                       stop=True)
                    ins.then_inc(full[b], 1)

            def transpose_result(name, i):
                for j in range(2):
                    wait_drained((i, j))
                    transpose(name, ev[:, i % 2, :], j)

            def compare_pairs(name, p):
                c0, c1 = PIECES[p]
                b = refill((name, p % 2))
                o = psum[b][0:N, 0:(c1 - c0) * N]
                t.matmul(o, ones[:, :], diag[:, c0:c1, :].rearrange("p c n -> p (c n)"), start=True, stop=False)
                t.matmul(o.rearrange("p (c n) -> p c n", n=N), ident_b[:, :],
                         tri_b[:, :].unsqueeze(1).to_broadcast([N, c1 - c0, N]), start=False, stop=True)\
                    .then_inc(full[b], 1)

            def pair_keys(name, p):
                c0, c1 = PIECES[p]
                b = refill((name, p % 2))
                for c in range(c0, c1):
                    ins = t.matmul(psum[b][0:N, (c - c0) * N:(c - c0 + 1) * N], oh_src[:, c, :], oh_key[:, c, :],
                                   start=True, stop=True)
                ins.then_inc(full[b], 1)

            pe.wait_ge(warm_ready, 1)
            keep_warm("h0T")
            pe.wait_ge(scaled, 1)
            aggregate("h0T", h, scaled_m[:, 0, :], layer=0)
            keep_warm("eqA")
            product(Q, 0, "h0T", end=2, last=False, opens=True)
            keep_warm("eqA", 1)
            product(Q, 0, "h0T", begin=2, end=6, last=False)
            pe.wait_ge(sel_ready, 1)
            pe.wait_ge(bias_lo, 1)
            bias(Q, opens=False)
            product(Q, 0, "h0T", begin=6)
            pe.wait_ge(ident_ready, 1)
            bias(K)
            product(K, 0, "h0T", end=2, last=False)
            pe.wait_ge(diag_ready, 1)
            pe.wait_ge(tri_ready, 1)
            for p in (0, 1):
                compare_pairs("eqA", p)
            product(K, 0, "h0T", begin=2, end=4, last=False)
            for p in (2, 3):
                compare_pairs("eqB", p)
            product(K, 0, "h0T", begin=4, end=6, last=False)
            transpose_result("qT", Q)
            product(K, 0, "h0T", begin=6)
            bias(V)
            product(V, 0, "h0T", end=2, last=False)
            for p, name in enumerate(("eqA", "eqA", "eqB", "eqB")):
                wait_drained((name, p % 2))
            b = refill(("voids", 0))
            for c in range(EC):
                ins = t.matmul(psum[b][0:N, c:c + 1], same[:, c, :], ones_b[:, :], start=True, stop=True)
            ins.then_inc(full[b], 1)
            product(V, 0, "h0T", begin=2, end=6, last=False)
            transpose_result("kT", K)
            product(V, 0, "h0T", begin=6)
            bias(Q2)
            product(Q2, 1, "qT", end=2, last=False)
            pe.wait_ge(onehots_ready, 2 * EC)
            pe.wait_ge(keys_ready, 1)
            for p in (0, 1):
                pair_keys("keyA", p)
            product(Q2, 1, "qT", begin=2, end=3, last=False)
            for p in (2, 3):
                pair_keys("keyB", p)
            product(Q2, 1, "qT", begin=3, end=4, last=False)
            b = refill(("counts", 0))
            for n, (lhs, rhs) in enumerate(((oh_src, oh_dst), (oh_dst, oh_src))):
                for c in range(EC):
                    ins = t.matmul(psum[b][0:N, n * N:(n + 1) * N], lhs[:, c, :], rhs[:, c, :], start=(c == 0),
                                   stop=(c == EC - 1))
            ins.then_inc(full[b], 1)
            product(Q2, 1, "qT", begin=4, end=6, last=False)
            transpose_result("vT", V)
            product(Q2, 1, "qT", begin=6)
            bias(K2)
            product(K2, 2, "kT", end=2, last=False)
            wait_drained(("counts", 0))
            b = refill(("degrees", 0))
            for n in range(2):
                t.matmul(psum[b][0:N, n * N:(n + 1) * N], ones[:, :], C[:, n, :], start=True, stop=True)
                ins = t.matmul(psum[b][0:N, 2 * N + n:2 * N + n + 1], C[:, n, :], ones[:, 0:1], start=True, stop=True)
            ins.then_inc(full[b], 1)
            product(K2, 2, "kT", begin=2, end=6, last=False)
            transpose_result("q2T", Q2)
            product(K2, 2, "kT", begin=6)
            bias(V2)
            product(V2, 0, "vT", end=2, last=False)
            transpose_result("k2T", K2)
            product(V2, 0, "vT", begin=2, end=3, last=False)
            pe.wait_ge(mask_ready, 1)
            for e in range(2):
                wait_drained(("q2T", e))
                wait_drained(("k2T", e))
                for j in range(2):
                    b = refill((f"scores{e}", j))
                    t.matmul(tview(b, N), ident[:, :], mask[:, :].unsqueeze(1).to_broadcast([N, HC, N]),
                             start=True, stop=False)
                    for c in range(HC):
                        rows, kk = slice(DH * j, DH * j + DH), HC * e + c
                        ins = t.matmul(psum[b][0:N, c * N:(c + 1) * N], q2T[rows, kk, :], k2T[rows, kk, :],
                                       start=False, stop=(c == HC - 1))
                    ins.then_inc(full[b], 1)
            product(V2, 0, "vT", begin=3)
            bias(O)
            for p in range(4):
                name = f"probsT{p // 2}"
                pe.wait_ge(probs_ready, p + 1)
                b = refill((name, p % 2))
                for c in range(4):
                    ins = t.transpose(psum[b][0:N, c * N:(c + 1) * N], S[:, 4 * p + c, :], ident[:, :])
                ins.then_inc(full[b], 1)
            for e in range(2):
                wait_drained((V2, e))
                for j in range(2):
                    wait_drained((f"probsT{e}", j))
                b = refill(("headsT", e))
                for c in range(HC):
                    for j in range(2):
                        head = 2 * (HC * e + c) + j
                        ins = t.matmul(psum[b][DH * j:DH * j + DH, c * N:(c + 1) * N],
                                       ev[:, V2 % 2, head * DH:(head + 1) * DH], PT[:, 8 * e + 4 * j + c, :],
                                       start=True, stop=True)
                ins.then_inc(full[b], 1)
            product(O, 1, "headsT")
            bias(SAGE0)
            keep_warm("h1T")
            pe.wait_ge(scaled, 2)
            aggregate("h1T", h, scaled_m[:, 0, :], layer=1)
            pe.wait_ge(scaled, 3)
            aggregate("mean1T", h, scaled_m[:, 1, :])
            product(SAGE0, 2, "h1T", last=False, end=4)
            pe.wait_ge(A23_ready, 1)
            b = refill(("rowsum", 0))
            t.matmul(psum[b][0:12, 0:N], bcol[:, :], A2T[:, :], start=True, stop=True).then_inc(full[b], 1)
            product(SAGE0, 2, "h1T", last=False, begin=4)
            product(SAGE0, 0, "mean1T", first=4)
            bias(SAGE1)
            keep_warm("hiddenT")
            transpose_result("hiddenT", SAGE0)
            aggregate("mean2T", ev[:, SAGE0 % 2, :], A1T[:, :])
            product(SAGE1, 1, "hiddenT", last=False)
            product(SAGE1, 2, "mean2T", first=4)
            bias(GCN2)
            keep_warm("h2T")
            pe.wait_ge(scaled, 4)
            aggregate("h2T", h, scaled_m[:, 0, :], layer=2)
            product(GCN2, 0, "h2T")
            bias(GCN3A)
            keep_warm("h3T")
            pe.wait_ge(scaled, 5)
            aggregate("h3T", h, scaled_m[:, 0, :], layer=3)
            b = FILL[GCN3A, 0][0]
            for k in range(KC):
                g = 2 * FIRST_UNIT[GCN3A] + k // 4
                if k % HC == 0:
                    wait_drained(("h3T", k // HC))
                    wait_split(g)
                r, c = g % RING, slice((k % 4) * F, (k % 4 + 1) * F)
                for n, (lhs, rhs) in enumerate(((a_hi, w_hi), (a_hi, w_lo), (a_lo, w_hi))):
                    ins = t.matmul(psum[b][0:N, 0:F], lhs[:, 1, k, :], rhs[:, r, c], start=False,
                                   stop=(k == KC - 1 and n == 2))
            ins.then_inc(full[b], 1)
            bias(GCN3B)
            wait_drained((GCN3A, 0))
            aggregate("gT", ev[:, GCN3A % 2, :], A3T[:, :], 1, 2)
            wait_drained(("gT", 0))
            for k in range(2):
                wait_split(2 * FIRST_UNIT[GCN3B] + k)
            for j in range(2):
                b = FILL[GCN3B, j][0]
                for k in range(2):
                    r = (2 * FIRST_UNIT[GCN3B] + k) % RING
                    for n, (lhs, rhs) in enumerate(((a_hi, w_hi), (a_hi, w_lo), (a_lo, w_hi))):
                        ins = t.matmul(psum[b][0:N, :], lhs[:, 2, k, :], rhs[:, r, hcols(j)], start=False,
                                       stop=(k == 1 and n == 2))
                ins.then_inc(full[b], 1)


WEIGHTS = [("L0_gnn_wq", True), ("L0_gnn_wk", True), ("L0_gnn_wv", True), ("L0_gnn_wiq", True), ("L0_gnn_wik", True),
           ("L0_gnn_wiv", True), ("L0_gnn_wo", True), ("L1_gnn_W_self0", False), ("L1_gnn_W_neigh0", False),
           ("L1_gnn_W_self1", False), ("L1_gnn_W_neigh1", False), ("L2_gnn_W", True), ("L3_gnn_W1", False),
           ("L3_gnn_W2", False)]
BIASES = ["L0_gnn_bq", "L0_gnn_bk", "L0_gnn_bv", "L0_gnn_biq", "L0_gnn_bik", "L0_gnn_biv", "L0_gnn_bo", "L1_gnn_b0",
          "L1_gnn_b1", "L2_gnn_b", "L3_gnn_b1", "L3_gnn_b2"]


def kernel(**inputs):
    import numpy as np
    import concourse.bacc as bacc
    from concourse.bass_utils import run_bass_kernel_spmd

    units = []
    for name, transposed in WEIGHTS:
        w = np.asarray(inputs[name])
        w = w.T if transposed else w
        rows, cols = w.shape
        per = UNIT // cols
        w = w.reshape(rows // (per * P), per, P, cols).transpose(0, 2, 1, 3)
        units.append(w.reshape(-1, P, UNIT))
    biases = np.zeros((12, D), np.float32)
    for n, name in enumerate(BIASES):
        b = np.asarray(inputs[name])
        biases[n, :b.shape[0]] = b
    edges = np.stack([np.asarray(inputs[k]).reshape(EC, N).T for k in ("src", "dst", "edge_type_5")], axis=1)
    arrays = {
        "x": np.ascontiguousarray(inputs["x"]), "weights": np.concatenate(units), "biases": biases,
        "edges": np.ascontiguousarray(edges), "edge_w": np.asarray(inputs["L0_gnn_edge_type_weights"]).reshape(1, 4),
    }
    nc = bacc.Bacc("TRN2", target_bir_lowering=False, num_devices=1)
    args = [nc.dram_tensor(f"in_{k}", a.shape, mybir.dt.from_np(a.dtype), kind="ExternalInput").ap()
            for k, a in arrays.items()]
    args.append(nc.dram_tensor("out_x", (N, D), mybir.dt.float32, kind="ExternalOutput").ap())
    gnn_kernel(nc, *args)
    r = run_bass_kernel_spmd(nc, [{f"in_{k}": a for k, a in arrays.items()}], core_ids=[0])
    return r.results[0]["out_x"]
```

```python
import concourse.bass as bass
from concourse import mybir
from contextlib import ExitStack

N, D, F = 96, 1024, 256
P = 128
KC = D // P
H, DH = 16, 64
NE, EC = 1632, 17
HB = D // 2
HC = KC // 2
TW = HC * N
SR, BR = 44, 76
LN_EPS = 1e-5
SCALE = 1.0 / DH ** 0.5
NO_EDGE = -1.0e30
PAIR = 128
TRI = 32768.0
UNITS, UNIT = 50, 2 * D
RAW, RING = 5, 10

Q, K, V, Q2, K2, V2, O, SAGE0, SAGE1, GCN2, GCN3A, GCN3B = range(12)
FIRST_UNIT = {Q: 0, K: 4, V: 8, Q2: 12, K2: 16, V2: 20, O: 24, SAGE0: 28, SAGE1: 36, GCN2: 44, GCN3A: 48, GCN3B: 49}

CHUNKS = 2 * UNITS
BY_DVE = 1
BY_POOL = (27, 30, 35, 43, 45, 53, 57, 59)
PASSED_LATER = (27, 35, 43, 45, 53, 57)
LOW_ORDER = list(range(CHUNKS))
for _s in PASSED_LATER:
    LOW_ORDER[_s:_s + 2] = _s + 1, _s
BEFORE = {i: 2 * u for i, u in FIRST_UNIT.items()}

EVENTS = [("h0T", 2), ("eqA", 2), ("eqB", 2), ("qT", 2), ("voids", 1), ("kT", 2), ("keyA", 2), ("keyB", 2),
          ("counts", 1), ("vT", 2), ("countsT", 1), ("degrees", 1), ("q2T", 2), ("k2T", 2), ("scores0", 2),
          ("scores1", 2), ("probsT0", 2), ("probsT1", 2), ("headsT", 2), ("mean1T", 2), ("h1T", 2), ("rowsum", 1),
          ("hiddenT", 2), ("mean2T", 2), ("h2T", 2), ("h3T", 2), ("gT", 1)]


def bank_fills():
    count, out = [0] * 8, {}
    for t, (name, halves) in enumerate(EVENTS):
        for j in range(halves):
            b = 4 + 2 * (t % 2) + j
            count[b] += 1
            out[name, j] = (b, count[b])
    return out


FILL = bank_fills()
for _i in range(12):
    for _j in range(2):
        FILL[_i, _j] = (2 * (_i % 2) + _j, _i // 2 + 1)

WARM = {"h0T": 10, "eqA": 3}

PIECES = [(0, 5), (5, 9), (9, 13), (13, 17)]
ACT_HI = ["h0T", "qT", "kT", "vT", "headsT", "mean1T", "h1T", "hiddenT", "mean2T", "h2T", "h3T", "gT"]
HI_COUNT = {}
for _name in ACT_HI:
    for _j in range(1 if _name == "gT" else 2):
        HI_COUNT[_name, _j] = len(HI_COUNT) + 1


def gnn_kernel(nc, x_in, weights, biases, edges, edge_w, out):
    f32, f32r, bf16, i32 = mybir.dt.float32, mybir.dt.float32r, mybir.dt.bfloat16, mybir.dt.int32
    ALU, ACT, AX = mybir.AluOpType, mybir.ActivationFunctionType, mybir.AxisListType
    ctx = ExitStack()
    with ctx:
        def sb(name, shape, dt=f32):
            return ctx.enter_context(nc.sbuf_tensor(name, shape, dt))

        def sem(name):
            return ctx.enter_context(nc.semaphore(name))

        raw = sb("raw", [P, RAW, 2, D])
        w_hi = sb("w_hi", [P, RING, D], f32r)
        w_lo = sb("w_lo", [P, RING, D], f32r)
        x = sb("x", [N, D])
        h = sb("h", [N, D])
        ev = sb("ev", [N, 2, D])
        a_hi = sb("a_hi", [P, 3, KC, N], f32r)
        a_lo = sb("a_lo", [P, 3, KC, N], f32r)
        q2T = sb("q2T", [P, KC, N])
        k2T = sb("k2T", [P, KC, N])
        S = sb("S", [N, EC, N])
        PT = sb("PT", [N, EC, N])
        onehot = PT[:, :, :].rearrange("p c n -> p (c n)").bitcast(bf16).rearrange("p (k c n) -> p k c n", k=2, c=EC)
        oh_src, oh_dst = onehot[:, 0], onehot[:, 1]
        diag = S[:, :, :].rearrange("p c n -> p (c n)").bitcast(bf16).rearrange("p (k c n) -> p k c n", k=2, c=EC)
        oh_key = sb("oh_key", [N, EC, N], bf16)
        same = oh_key
        b_parts = sb("b_parts", [BR, D], f32r)
        b_raw = ev[0:BR, 1, :]
        sel = sb("sel", [SR, 12, N], f32r)
        sel_f = S[0:SR, 0:12, :]
        rs = sb("rs", [BR, N], f32r)
        warm = sb("warm", [P, HB], bf16)
        ident = sb("ident", [N, N])
        ident_b = sb("ident_b", [N, N], bf16)
        ones = sb("ones", [N, N])
        ones_b = sb("ones_b", [N, N], bf16)
        tri_b = sb("tri_b", [N, N], bf16)
        iota_i = sb("iota_i", [N, N], i32)
        iota_f = sb("iota_f", [N, N])
        bcol = sb("bcol", [N, 12])
        edges_i = sb("edges_i", [N, 3, EC], i32)
        edges_f = sb("edges_f", [N, 3, EC])
        src, dst, typ = (edges_f[:, n, :] for n in range(3))
        src_pair = sb("src_pair", [N, EC])
        pair = sb("pair", [N, EC])
        key_i = sb("key_i", [N, EC], i32)
        key = sb("key", [N, EC])
        live = sb("live", [N, EC])
        kmax = sb("kmax", [N, 4, N])
        kind_i = sb("kind_i", [N, 2, N], i32)
        kind = sb("kind", [N, N])
        mterm = sb("mterm", [N, 3, N])
        mask = sb("mask", [N, N])
        mask_parts = sb("mask_parts", [N, 2, N], f32r)
        ident_r = sb("ident_r", [N, N], f32r)
        ew = sb("ew", [N, 4])
        ews = sb("ews", [N, 4, 4])
        C = sb("C", [N, 2, N])
        deg = sb("deg", [N, 2 * N + 2])
        dis = sb("dis", [N, 2, 2 * N + 2])
        mdeg = sb("mdeg", [N, 2, N])
        A1T = sb("A1T", [N, N])
        A2T = sb("A2T", [N, N])
        A3T = sb("A3T", [N, N])
        atmp = sb("atmp", [N, 4, N])
        stats = sb("stats", [N, 2, 6])
        mv = sb("mv", [N, 2])
        std = sb("std", [N, 2])
        eps = sb("eps", [N, 1])
        early = sb("early", [N, 1])
        token = [sb(f"token{n}", [N, 1]) for n in range(len(BY_POOL))]
        scaled_m = sb("scaled_m", [N, N])
        h_std = sb("h_std", [N, D])
        nmax = sb("nmax", [N, H])
        rsum = sb("rsum", [N, 2, H])
        psum = [ctx.enter_context(nc.psum_tensor(f"bank{b}", [P, HB], f32)) for b in range(8)]

        x_loaded = [sem(f"x_loaded{j}") for j in range(2)]
        edges_loaded, biases_loaded, ew_loaded = sem("edges_loaded"), sem("biases_loaded"), sem("ew_loaded")
        raw_loaded = [sem(f"raw_loaded{r}") for r in range(RAW)]
        raw_used = [sem(f"raw_used{r}") for r in range(RAW)]
        hi_ready = sem("hi_ready")
        pool_lo = sem("pool_lo")
        first_hi = sem("first_hi")
        ring_free = sem("ring_free")
        full = [sem(f"full{b}") for b in range(8)]
        drained = [sem(f"drained{b}") for b in range(8)]
        act_hi = sem("act_hi")
        centered = sem("centered")
        scaled = sem("scaled")
        h_scaled = sem("h_scaled")
        eps_ready, var_ready, std_ready = sem("eps_ready"), sem("var_ready"), sem("std_ready")
        cleared, bias_hi, bias_lo = sem("cleared"), sem("bias_hi"), sem("bias_lo")
        warm_ready, sel_f_ready, sel_ready, ident_ready = sem("warm_ready"), sem("sel_f_ready"), sem("sel_ready"), sem("ident_ready")
        diag_ready, tri_ready, live_ready = sem("diag_ready"), sem("tri_ready"), sem("live_ready")
        onehots_ready, keys_ready = sem("onehots_ready"), sem("keys_ready")
        kind_ready, ew_ready, mask_ready = sem("kind_ready"), sem("ew_ready"), sem("mask_ready")
        mdeg_ready, sdeg_ready, dis_ready = sem("mdeg_ready"), sem("sdeg_ready"), sem("dis_ready")
        A1_ready, A23_ready = sem("A1_ready"), sem("A23_ready")
        max_ready, exp_ready, inverse_ready = sem("max_ready"), sem("exp_ready"), sem("inverse_ready")
        probs_ready = sem("probs_ready")
        pool_step, dve_step, act_step = sem("pool_step"), sem("dve_step"), sem("act_step")
        left_ready, right_ready, stored = sem("left_ready"), sem("right_ready"), sem("stored")
        x_kept = sem("x_kept")

        def tcols(j):
            return slice(j * HC, (j + 1) * HC)

        def hcols(j):
            return slice(j * HB, (j + 1) * HB)

        def tview(b, rows=P, k=HC):
            return psum[b][0:rows, 0:k * N].rearrange("p (c n) -> p c n", n=N)

        block = ctx.enter_context(nc.Block())

        @block.sync
        def _(sp):
            for j in range(2):
                sp.dma_start(x[:, hcols(j)], x_in[:, hcols(j)]).then_inc(x_loaded[j], 16)

            def load(u, r):
                sp.dma_start(raw[:, r, :, :].rearrange("p c n -> p (c n)"), weights[u]).then_inc(raw_loaded[r], 16)

            load(0, 0)
            sp.dma_start(edges_i[:, :, :], edges).then_inc(edges_loaded, 16)
            sp.wait_ge(cleared, 1)
            for p in (0, 32, 64):
                sp.dma_start(b_raw[p:p + 12, :], biases).then_inc(biases_loaded, 16)
            sp.dma_start(ew[:, :], edge_w.to_broadcast([N, 4])).then_inc(ew_loaded, 16)
            for r in range(1, RAW):
                load(r, r)
            with sp.Fori(1, UNITS // RAW) as turn:
                for r in range(RAW):
                    sp.wait_ge(raw_used[r], turn * 2)
                    load(turn * RAW + r, r)
            for j in range(2):
                sp.wait_ge((left_ready, right_ready)[j], 1)
                sp.dma_start(out[:, hcols(j)], x[:, hcols(j)]).then_inc(stored, 16)
            sp.wait_ge(stored, 32)

        @block.gpsimd
        def _(pool):
            steps, low = [0], [0]

            def weights_lo(count):
                for s in BY_POOL[low[0]:low[0] + count]:
                    u, c = divmod(s, 2)
                    pool.wait_ge(hi_ready, s - BY_DVE + 1)
                    nc.gpsimd.tensor_tensor(w_lo[:, s % RING, :], raw[:, u % RAW, c, :],
                                            w_hi[:, s % RING, :].bitcast(f32), ALU.subtract).then_inc(pool_lo, 1)
                low[0] += count
                pool.wait_ge(pool_lo, low[0])

            def step(ins):
                steps[0] += 1
                ins.then_inc(pool_step, 1)
                pool.wait_ge(pool_step, steps[0])

            g = nc.gpsimd
            step(g.memset(ident[:, :], 0.0))
            g.affine_select(out=ident[:, :], in_=ident[:, :], compare_op=ALU.not_equal, fill=1.0, base=0,
                            pattern=[[-1, N]], channel_multiplier=1).then_inc(ident_ready, 1)
            step(g.memset(sel_f, 0.0))
            for base in (0, 32):
                ins = g.affine_select(out=sel_f, in_=sel_f, compare_op=ALU.not_equal, fill=1.0, base=base,
                                      pattern=[[1, 12], [0, N]], channel_multiplier=-1)
                if base == 0:
                    step(ins)
                else:
                    ins.then_inc(sel_f_ready, 1)
            step(g.iota(iota_i[:, :], [[1, N]], base=0, channel_multiplier=0))
            step(g.tensor_copy(iota_f[:, :], iota_i[:, :]))
            step(g.iota(key_i[:, :], [[8, EC]], base=1, channel_multiplier=0))
            step(g.tensor_copy(key[:, :], key_i[:, :]))
            pool.wait_ge(edges_loaded, 16)
            step(g.tensor_copy(edges_f[:, :, :], edges_i[:, :, :]))
            step(g.tensor_scalar(src_pair[:, :], src, float(PAIR), 0.0, ALU.mult, ALU.add))
            step(g.tensor_tensor(pair[:, :], src_pair[:, :], dst, ALU.add))
            step(g.tensor_tensor(key[:, :], key[:, :], typ, ALU.add))
            pool.wait_ge(sel_ready, 1)
            pool.wait_ge(ident_ready, 1)
            for n, part in enumerate((src_pair[:, :], dst)):
                g.tensor_tensor(diag[:, n, :, :], ident[:, :].unsqueeze(1).to_broadcast([N, EC, N]),
                                part.unsqueeze(2).to_broadcast([N, EC, N]), ALU.mult).then_inc(diag_ready, 1)
                pool.wait_ge(diag_ready, n + 1)
                if n == 0:
                    pool.wait_ge(bias_hi, 1)
                    g.tensor_tensor(b_parts[32:SR, :], b_raw[32:SR, :], b_parts[32:SR, :].bitcast(f32), ALU.subtract)\
                        .then_inc(bias_lo, 1)
                    pool.wait_ge(bias_lo, 1)
            step(g.tensor_copy(ident_b[:, :], ident[:, :]))
            step(g.memset(ones[:, :], 1.0))
            step(g.tensor_copy(ones_b[:, :], ones[:, :]))
            step(g.affine_select(out=tri_b[:, :], in_=ones[:, :], compare_op=ALU.is_ge, fill=0.0, base=0,
                                 pattern=[[1, N]], channel_multiplier=-1))
            g.tensor_scalar(tri_b[:, :], tri_b[:, :], TRI, 1.0, ALU.mult, ALU.mult).then_inc(tri_ready, 1)
            step(g.memset(bcol[:, :], 0.0))
            step(g.memset(bcol[:, GCN2:GCN2 + 1], 1.0))
            for c in range(EC):
                g.tensor_scalar(oh_src[:, c, :], iota_f[:, :], src[:, c:c + 1], None, ALU.is_equal)\
                    .then_inc(onehots_ready, 1)
                g.tensor_scalar(oh_dst[:, c, :], iota_f[:, :], dst[:, c:c + 1], None, ALU.is_equal)\
                    .then_inc(onehots_ready, 1)
            pool.wait_ge(onehots_ready, 2 * EC)
            pool.wait_ge(live_ready, 1)
            g.tensor_tensor(oh_key[:, :, :], oh_dst, live[:, :].unsqueeze(2).to_broadcast([N, EC, N]), ALU.mult)\
                .then_inc(keys_ready, 1)
            weights_lo(3)
            pool.wait_ge(kind_ready, 1)
            pool.wait_ge(ew_ready, 1)
            none, off, on = (mterm[:, n, :] for n in range(3))
            w = ews[:, 3, :]
            step(g.tensor_scalar(none, kind[:, :], 0.0, None, ALU.is_equal))
            step(g.tensor_tensor(on, none, ident[:, :], ALU.mult))
            step(g.tensor_tensor(off, none, on, ALU.subtract))
            step(g.tensor_scalar(off, off, NO_EDGE, 0.0, ALU.mult, ALU.add))
            step(g.tensor_scalar(on, on, w[:, 3:4], 0.0, ALU.mult, ALU.add))
            step(g.tensor_tensor(mask[:, :], off, on, ALU.add))
            for k, m in ((1, 3), (2, 0), (3, 1), (4, 2), (5, 3)):
                step(g.tensor_scalar(on, kind[:, :], float(k), w[:, m:m + 1], ALU.is_equal, ALU.mult))
                ins = g.tensor_tensor(mask[:, :], mask[:, :], on, ALU.add)
                step(ins)
            step(g.tensor_copy(mask_parts[:, 0, :], mask[:, :]))
            step(g.tensor_tensor(mask_parts[:, 1, :], mask[:, :], mask_parts[:, 0, :].bitcast(f32), ALU.subtract))
            g.tensor_copy(ident_r[:, :], ident[:, :]).then_inc(mask_ready, 1)
            pool.wait_ge(mdeg_ready, 1)
            g.tensor_tensor(A1T[:, :], C[:, 0, :], mdeg[:, 1, :], ALU.mult).then_inc(A1_ready, 1)
            weights_lo(2)
            for p in range(4):
                heads = slice(4 * p, 4 * p + 4)
                pool.wait_ge(inverse_ready, p + 1)
                g.tensor_tensor(S[:, heads, :], S[:, heads, :],
                                rsum[:, 1, heads].unsqueeze(2).to_broadcast([N, 4, N]), ALU.mult)\
                    .then_inc(probs_ready, 1)
            weights_lo(3)
            pool.wait_ge(dis_ready, 1)
            for k, (cc, AT) in enumerate(((1, A2T), (0, A3T))):
                by = 1 - k
                step(g.tensor_tensor(atmp[:, 2 * k, :], C[:, cc, :], ident[:, :], ALU.add))
                step(g.tensor_tensor(atmp[:, 2 * k + 1, :], atmp[:, 2 * k, :], dis[:, 1, by * N:(by + 1) * N], ALU.mult))
                g.tensor_scalar(AT[:, :], atmp[:, 2 * k + 1, :], dis[:, 1, 2 * N + by:2 * N + by + 1], 0.0,
                                ALU.mult, ALU.add).then_inc(A23_ready, 1)

        @block.scalar
        def _(act):
            a = nc.scalar
            steps, done = [0], [BY_DVE]

            def step(ins):
                steps[0] += 1
                ins.then_inc(act_step, 1)
                act.wait_ge(act_step, steps[0])

            def weights_hi(upto):
                while done[0] < min(upto, CHUNKS):
                    s = done[0]
                    u, c = divmod(s, 2)
                    if c == 0 or s == BY_DVE:
                        act.wait_ge(raw_loaded[u % RAW], 16 * (u // RAW + 1))
                    if s >= RING:
                        act.wait_ge(ring_free, s - RING + 1)
                    a.activation(w_hi[:, s % RING, :], raw[:, u % RAW, c, :], ACT.Copy).then_inc(hi_ready, 1)
                    done[0] += 1

            def wait_full(key):
                b, n = FILL[key]
                act.wait_ge(full[b], n)
                return b

            def copy_out(i, halves=(0, 1), func=ACT.Copy, cols=HB):
                for j in halves:
                    b = wait_full((i, j))
                    a.activation(ev[:, i % 2, j * HB:j * HB + cols], psum[b][0:N, 0:cols], func)\
                        .then_inc(drained[b], 1)

            def acts_hi(name, slot, halves=(0, 1), k=HC):
                for j in halves:
                    b = wait_full((name, j))
                    a.activation(a_hi[:, slot, j * HC:j * HC + k, :], tview(b, k=k), ACT.Copy).then_inc(act_hi, 1)

            def transposed_out(name, j, tile, scale=1.0):
                b = wait_full((name, j))
                a.activation(tile[:, tcols(j), :], tview(b), ACT.Copy, scale=scale).then_inc(drained[b], 1)

            def norm(layer, i=None):
                for j in range(0 if i is None else 2):
                    b, n = FILL[i, j]
                    act.wait_ge(drained[b], n)
                    a.activation(x[:, hcols(j)], psum[b][0:N, :], ACT.Copy).then_inc(x_kept, 1)
                act.wait_ge(var_ready, layer + 1)
                a.activation(std[:, 0:1], mv[:, 1:2], ACT.Sqrt, bias=eps[:, :]).then_inc(std_ready, 1)

            act.wait_ge(eps_ready, 1)
            a.activation(early[:, :], eps[:, :], ACT.Sqrt)
            norm(0)
            act.wait_ge(sel_f_ready, 1)
            a.activation(sel[:, :, :], sel_f, ACT.Copy).then_inc(sel_ready, 1)
            acts_hi("h0T", 0, (0,))
            weights_hi(2)
            acts_hi("h0T", 0, (1,))
            act.wait_ge(biases_loaded, 48)
            a.activation(b_parts[:, :], b_raw, ACT.Copy).then_inc(bias_hi, 1)
            weights_hi(BEFORE[K] + 2)
            copy_out(Q)
            weights_hi(BEFORE[V] + 1)
            acts_hi("qT", 1)
            weights_hi(BEFORE[V] + 4)
            copy_out(K)
            weights_hi(BEFORE[Q2] + 3)
            acts_hi("kT", 2)
            weights_hi(BEFORE[Q2] + 5)
            copy_out(V)
            weights_hi(BEFORE[Q2] + 8)
            act.wait_ge(ew_loaded, 16)
            step(a.activation(ews[:, 0, :], ew[:, :], ACT.Abs))
            step(a.activation(ews[:, 1, :], ews[:, 0, :], ACT.Exp, scale=-1.0))
            step(a.activation(ews[:, 2, :], ews[:, 1, :], ACT.Ln, bias=1.0))
            weights_hi(BEFORE[K2] + 4)
            acts_hi("vT", 0)
            weights_hi(BEFORE[K2] + 5)
            copy_out(Q2)
            weights_hi(BEFORE[V2] + 4)
            transposed_out("q2T", 0, q2T, SCALE)
            transposed_out("q2T", 1, q2T, SCALE)
            weights_hi(BEFORE[V2] + 6)
            copy_out(K2)
            transposed_out("k2T", 0, k2T)
            weights_hi(BEFORE[V2] + 7)
            for p in range(4):
                b, _ = FILL[f"scores{p // 2}", p % 2]
                act.wait_ge(max_ready, p + 1)
                for c in range(4):
                    hh = 4 * p + c
                    a.activation(S[:, hh, :], psum[b][0:N, c * N:(c + 1) * N], ACT.Exp, bias=nmax[:, hh:hh + 1],
                                 accum_out=rsum[:, 0, hh:hh + 1]).then_inc(exp_ready if c < 3 else drained[b], 1)
                weights_hi(BEFORE[V2] + (8, 8, 9, 10)[p])
            for p in (0, 2):
                if p == 2:
                    copy_out(V2, (0,))
                    weights_hi(BEFORE[O] + 3)
                b = wait_full((f"probsT{p // 2}", p % 2))
                a.activation(PT[:, 4 * p:4 * p + 4, :], tview(b, N), ACT.Copy).then_inc(drained[b], 1)
            acts_hi("headsT", 1)
            weights_hi(BEFORE[SAGE0] + 3)
            norm(1)
            for j in range(2):
                act.wait_ge(scaled, 2)
                act.wait_ge(centered, 3 + j)
                a.activation(h_std[:, hcols(j)], h[:, hcols(j)], ACT.Copy, scale=std[:, 1:2]).then_inc(h_scaled, 1)
            acts_hi("mean1T", 0)
            weights_hi(BEFORE[SAGE0] + 4)
            acts_hi("h1T", 2)
            b, n = FILL["degrees", 0]
            act.wait_ge(drained[b], n)
            a.activation(dis[:, 0, :], deg[:, :], ACT.Sqrt).then_inc(sdeg_ready, 1)
            weights_hi(BEFORE[SAGE1] + 3)
            copy_out(SAGE0, (0,), ACT.Relu)
            weights_hi(BEFORE[SAGE1] + 3)
            acts_hi("hiddenT", 1)
            acts_hi("mean2T", 2)
            weights_hi(BEFORE[GCN2] + 3)
            norm(2, SAGE1)
            weights_hi(BEFORE[GCN2] + 4)
            acts_hi("h2T", 0)
            weights_hi(BEFORE[GCN3A] + 3)
            norm(3, GCN2)
            acts_hi("h3T", 1)
            weights_hi(CHUNKS)
            copy_out(GCN3A, (0,), ACT.Relu, F)
            acts_hi("gT", 2, (0,), 2)
            b = wait_full((GCN3B, 1))
            a.activation(x[:, hcols(1)], psum[b][0:N, :], ACT.Copy).then_inc(right_ready, 1)

        @block.vector
        def _(dve):
            v = nc.vector
            steps, done = [0], [0]

            def step(ins):
                steps[0] += 1
                ins.then_inc(dve_step, 1)
                dve.wait_ge(dve_step, steps[0])

            def weights_lo(upto):
                while done[0] < min(upto, CHUNKS):
                    s = LOW_ORDER[done[0]]
                    u, c = divmod(s, 2)
                    done[0] += 1
                    if s in BY_POOL:
                        dve.wait_ge(pool_lo, BY_POOL.index(s) + 1)
                        v.memset(token[BY_POOL.index(s)][:, :], 0.0).then_inc(raw_used[u % RAW], 1)
                        continue
                    if s < BY_DVE:
                        dve.wait_ge(first_hi, s + 1)
                    else:
                        dve.wait_ge(hi_ready, s - BY_DVE + 1)
                    v.tensor_tensor(w_lo[:, s % RING, :], raw[:, u % RAW, c, :], w_hi[:, s % RING, :].bitcast(f32),
                                    ALU.subtract).then_inc(raw_used[u % RAW], 1)

            def wait_full(key):
                b, n = FILL[key]
                dve.wait_ge(full[b], n)
                return b

            def copy_out(i, j):
                b = wait_full((i, j))
                v.tensor_copy(ev[:, i % 2, hcols(j)], psum[b][0:N, :]).then_inc(drained[b], 1)

            def acts_lo(name, slot, halves=(0, 1), k=HC):
                for j in halves:
                    b, _ = FILL[name, j]
                    dve.wait_ge(act_hi, HI_COUNT[name, j])
                    v.tensor_tensor(a_lo[:, slot, j * HC:j * HC + k, :], tview(b, k=k),
                                    a_hi[:, slot, j * HC:j * HC + k, :].bitcast(f32), ALU.subtract)\
                        .then_inc(drained[b], 1)

            def transposed_out(name, j, tile):
                b = wait_full((name, j))
                v.tensor_copy(tile[:, tcols(j), :], tview(b)).then_inc(drained[b], 1)

            def statistics(i):
                for j in range(2):
                    b = wait_full((i, j))
                    v.bn_stats(stats[:, j, :], psum[b][0:N, :]).then_inc(drained[b], 1)
                for j in range(2):
                    b, n = FILL[i, j]
                    dve.wait_ge(drained[b], n)

            def residual(i):
                for j in range(2):
                    b = wait_full((i, j))
                    v.tensor_tensor(x[:, hcols(j)], psum[b][0:N, :], x[:, hcols(j)], ALU.add).then_inc(drained[b], 1)
                    dve.wait_ge(drained[b], FILL[i, j][1])
                    steps[0] += 1
                    v.bn_stats(stats[:, j, :], x[:, hcols(j)]).then_inc(dve_step, 1)
                dve.wait_ge(dve_step, steps[0])

            def norm(layer, M):
                v.bn_aggr(mv[:, :], stats[:, :, :].rearrange("p a b -> p (a b)")).then_inc(var_ready, 1)
                dve.wait_ge(var_ready, layer + 1)
                if layer > 1:
                    dve.wait_ge(x_kept, 2 * layer - 3)
                v.tensor_scalar(h[:, hcols(0)], x[:, hcols(0)], mv[:, 0:1], 0.0, ALU.subtract, ALU.max)\
                    .then_inc(centered, 1)
                dve.wait_ge(std_ready, layer + 1)
                step(v.reciprocal(std[:, 1:2], std[:, 0:1]))
                v.tensor_scalar(scaled_m[:, :], M[:, :], std[:, 1:2], None, ALU.mult).then_inc(scaled, 1)
                if layer > 1:
                    dve.wait_ge(x_kept, 2 * layer - 2)
                v.tensor_scalar(h[:, hcols(1)], x[:, hcols(1)], mv[:, 0:1], 0.0, ALU.subtract, ALU.max)\
                    .then_inc(centered, 1)

            v.memset(eps[:, :], LN_EPS).then_inc(eps_ready, 1)
            v.memset(warm[:, :], 0.0).then_inc(warm_ready, 1)
            v.memset(b_raw, 0.0).then_inc(cleared, 1)
            step(v.memset(rs[:, :].bitcast(f32), 0.0))
            for j in range(2):
                dve.wait_ge(x_loaded[j], 16)
                step(v.bn_stats(stats[:, j, :], x[:, hcols(j)]))
            dve.wait_ge(ident_ready, 1)
            norm(0, ident)
            dve.wait_ge(raw_loaded[0], 16)
            for s in range(BY_DVE):
                v.tensor_copy(w_hi[:, s, :], raw[:, 0, s, :]).then_inc(first_hi, 1)
            weights_lo(1)
            acts_lo("h0T", 0, (0,))
            weights_lo(2)
            acts_lo("h0T", 0, (1,))
            weights_lo(BEFORE[K] + 4)

            def mark_same(name, p):
                c0, c1 = PIECES[p]
                b = wait_full((name, p % 2))
                v.tensor_tensor(same[:, c0:c1, :], tview(b, N, c1 - c0),
                                pair[:, c0:c1].unsqueeze(2).to_broadcast([N, c1 - c0, N]), ALU.is_equal)\
                    .then_inc(drained[b], 1)

            dve.wait_ge(diag_ready, 2)
            mark_same("eqA", 0)
            mark_same("eqA", 1)
            weights_lo(BEFORE[K] + 6)
            mark_same("eqB", 2)
            mark_same("eqB", 3)
            weights_lo(BEFORE[V] + 1)
            acts_lo("qT", 1)
            weights_lo(BEFORE[V] + 4)
            b = wait_full(("voids", 0))
            v.tensor_scalar(live[:, :], psum[b][0:N, 0:EC], 0.0, None, ALU.is_equal).then_inc(drained[b], 1)
            dve.wait_ge(drained[b], FILL["voids", 0][1])
            v.tensor_tensor(live[:, :], live[:, :], key[:, :], ALU.mult).then_inc(live_ready, 1)
            weights_lo(BEFORE[Q2] + 2)
            acts_lo("kT", 2)

            def last_keys(name, p):
                c0, c1 = PIECES[p]
                b = wait_full((name, p % 2))
                v.tensor_reduce(out=kmax[:, p, :], in_=tview(b, N, c1 - c0).rearrange("p c d -> p d c"), axis=AX.X,
                                op=ALU.max).then_inc(drained[b], 1)

            weights_lo(BEFORE[Q2] + 6)
            last_keys("keyA", 0)
            last_keys("keyA", 1)
            last_keys("keyB", 2)
            last_keys("keyB", 3)
            weights_lo(BEFORE[Q2] + 8)
            for p in range(4):
                b, n = FILL[("keyA", "keyB")[p // 2], p % 2]
                dve.wait_ge(drained[b], n)
            step(v.tensor_tensor(kmax[:, 0:2, :], kmax[:, 0:2, :], kmax[:, 2:4, :], ALU.max))
            step(v.tensor_tensor(kmax[:, 0, :], kmax[:, 0, :], kmax[:, 1, :], ALU.max))
            step(v.tensor_copy(kind_i[:, 0, :], kmax[:, 0, :]))
            step(v.tensor_scalar(kind_i[:, 1, :], kind_i[:, 0, :], 7, None, ALU.bitwise_and))
            v.tensor_copy(kind[:, :], kind_i[:, 1, :]).then_inc(kind_ready, 1)
            dve.wait_ge(act_step, 3)
            v.scalar_tensor_tensor(ews[:, 3, :], ew[:, :], 0.0, ews[:, 2, :], ALU.max, ALU.add).then_inc(ew_ready, 1)
            b = wait_full(("counts", 0))
            v.tensor_copy(C[:, 0, :], psum[b][0:N, 0:N]).then_inc(drained[b], 1)
            weights_lo(BEFORE[K2] + 2)
            acts_lo("vT", 0)
            weights_lo(BEFORE[K2] + 5)
            b = wait_full(("countsT", 0))
            v.tensor_copy(C[:, 1, :], psum[b][0:N, 0:N]).then_inc(drained[b], 1)
            weights_lo(BEFORE[K2] + 7)
            b = wait_full(("degrees", 0))
            step(v.tensor_scalar(mdeg[:, 0, :], psum[b][0:N, 0:N], 1.0, None, ALU.max))
            v.reciprocal(mdeg[:, 1, :], mdeg[:, 0, :]).then_inc(mdeg_ready, 1)
            v.tensor_scalar(deg[:, :], psum[b][0:N, 0:2 * N + 2], 1.0, None, ALU.add).then_inc(drained[b], 1)
            weights_lo(BEFORE[V2] + 5)
            transposed_out("k2T", 1, k2T)
            def sums_inverted(p):
                heads = slice(4 * p, 4 * p + 4)
                dve.wait_ge(exp_ready, 3 * p + 3)
                b, n = FILL[f"scores{p // 2}", p % 2]
                dve.wait_ge(drained[b], n)
                v.reciprocal(rsum[:, 1, heads], rsum[:, 0, heads]).then_inc(inverse_ready, 1)

            for p in range(4):
                b = wait_full((f"scores{p // 2}", p % 2))
                v.tensor_reduce(out=nmax[:, 4 * p:4 * p + 4], in_=tview(b, N), axis=AX.X, op=ALU.max, negate=True)\
                    .then_inc(max_ready, 1)
                if p >= 1:
                    weights_lo(BEFORE[V2] + min(6 + p, 8))
                    sums_inverted(p - 1)
            weights_lo(BEFORE[V2] + 9)
            sums_inverted(3)
            for p in (1, 3):
                if p == 3:
                    weights_lo(BEFORE[V2] + 10)
                    copy_out(V2, 1)
                b = wait_full((f"probsT{p // 2}", p % 2))
                v.tensor_copy(PT[:, 4 * p:4 * p + 4, :], tview(b, N)).then_inc(drained[b], 1)
            acts_lo("headsT", 1)
            weights_lo(BEFORE[SAGE0] + 1)
            residual(O)
            dve.wait_ge(A1_ready, 1)
            norm(1, A1T)
            weights_lo(BEFORE[SAGE0] + 2)
            acts_lo("mean1T", 0)
            weights_lo(BEFORE[SAGE0] + 3)
            acts_lo("h1T", 2)
            dve.wait_ge(sdeg_ready, 1)
            v.reciprocal(dis[:, 1, :], dis[:, 0, :]).then_inc(dis_ready, 1)
            weights_lo(BEFORE[SAGE0] + 10)
            b = wait_full(("rowsum", 0))
            for p in (0, 32):
                step(v.tensor_copy(rs[p:p + 12, :], psum[b][0:12, 0:N]))
            v.tensor_tensor(rs[64:76, :], psum[b][0:12, 0:N], rs[0:12, :].bitcast(f32), ALU.subtract)\
                .then_inc(drained[b], 1)
            weights_lo(BEFORE[SAGE1] + 2)
            b = wait_full((SAGE0, 1))
            v.tensor_scalar(ev[:, SAGE0 % 2, hcols(1)], psum[b][0:N, :], 0.0, None, ALU.max).then_inc(drained[b], 1)
            weights_lo(BEFORE[SAGE1] + 3)
            acts_lo("hiddenT", 1)
            acts_lo("mean2T", 2)
            weights_lo(BEFORE[GCN2] + 2)
            statistics(SAGE1)
            dve.wait_ge(A23_ready, 2)
            norm(2, A2T)
            weights_lo(BEFORE[GCN2] + 4)
            acts_lo("h2T", 0)
            weights_lo(BEFORE[GCN3A] + 2)
            statistics(GCN2)
            norm(3, A3T)
            weights_lo(BEFORE[GCN3A] + 3)
            acts_lo("h3T", 1)
            weights_lo(CHUNKS)
            acts_lo("gT", 2, (0,), 2)
            b = wait_full((GCN3B, 0))
            v.tensor_copy(x[:, hcols(0)], psum[b][0:N, :]).then_inc(left_ready, 1)

        @block.tensor
        def _(pe):
            t = nc.tensor
            owed = [False]

            def refill(key):
                b, n = FILL[key]
                if n > 1:
                    pe.wait_ge(drained[b], n - 1)
                return b

            def wait_drained(key):
                b, n = FILL[key]
                pe.wait_ge(drained[b], n)

            def bias(i, opens=True):
                halves, cols = (1, F) if i == GCN3A else (2, HB)
                for j in range(halves):
                    b = refill((i, j))
                    if i == GCN2:
                        if j == 0:
                            wait_drained(("rowsum", 0))
                        lhs, rows = rs[:, :], BR
                    else:
                        lhs, rows = sel[:, i, :], SR
                    ins = t.matmul(psum[b][0:N, 0:cols], lhs, b_parts[0:rows, j * HB:j * HB + cols], start=opens,
                                   stop=False)
                    if owed[0]:
                        ins.then_inc(ring_free, 1)
                        owed[0] = False

            def residual(i, layer, opens):
                for j in range(2):
                    b = refill((i, j))
                    if layer == 1:
                        wait_drained((O, j))
                    else:
                        pe.wait_ge(x_kept, 2 * layer - 3 + j)
                    t.matmul(psum[b][0:N, :], ident[:, :], x[:, hcols(j)], start=opens, stop=False)

            def keep_warm(name, count=None):
                b = refill((name, 0))
                for _ in range(count or WARM[name]):
                    t.matmul(psum[b][0:N, :], warm[:, 0:N], warm[:, :], start=True, stop=True)

            def wait_high(key):
                pe.wait_ge(act_hi, HI_COUNT[key])

            def product(i, slot, ready, first=0, last=True, begin=0, end=KC, opens=False, tail=2):
                g0 = 2 * (FIRST_UNIT[i] + first)
                banks = [FILL[i, j][0] for j in range(2)]

                def term(k, n, j, start=False, stop=False):
                    lhs, rhs = ((a_hi, w_hi), (a_hi, w_lo), (a_lo, w_hi))[n]
                    return t.matmul(psum[banks[j]][0:N, :], lhs[:, slot, k, :], rhs[:, (g0 + k) % RING, hcols(j)],
                                    start=start, stop=stop)

                k = begin
                while k < end:
                    if k % HC == 0 and k > 0:
                        wait_drained((ready, k // HC))
                    if k == 0:
                        wait_high((ready, 0))
                        for kk in (0, 1):
                            wait_split(g0 + kk)
                            for n in (0, 1):
                                for j in range(2):
                                    term(kk, n, j, start=opens and kk == n == 0)
                        wait_drained((ready, 0))
                        for kk in (0, 1):
                            for j in range(2):
                                ins = term(kk, 2, j)
                            ins.then_inc(ring_free, 1)
                        k += 2
                    elif last and k == KC - tail:
                        for kk in range(k, KC):
                            wait_split(g0 + kk)
                        for j in range(2):
                            for kk in range(k, KC):
                                for n in range(3):
                                    ins = term(kk, n, j, stop=(kk == KC - 1 and n == 2))
                                if kk < KC - 1 and j == 1:
                                    ins.then_inc(ring_free, 1)
                            ins.then_inc(full[banks[j]], 1)
                        owed[0] = True
                        k = KC
                    else:
                        wait_split(g0 + k)
                        for n in range(3):
                            for j in range(2):
                                ins = term(k, n, j)
                        ins.then_inc(ring_free, 1)
                        k += 1

            def wait_split(g):
                u, c = divmod(g, 2)
                pe.wait_ge(raw_used[u % RAW], 2 * (u // RAW) + c + 1)

            def transpose(name, tile, j):
                b = refill((name, j))
                for c in range(HC):
                    k = j * HC + c
                    ins = t.transpose(psum[b][:, c * N:(c + 1) * N], tile[:, k * P:(k + 1) * P], ident[:, :])
                ins.then_inc(full[b], 1)

            def aggregate(name, tile, AT, halves=2, k=HC, layer=None):
                for j in range(halves):
                    if layer is not None:
                        pe.wait_ge(centered, 2 * layer + j + 1)
                    b = refill((name, j))
                    for c in range(k):
                        kk = j * HC + c
                        ins = t.matmul(psum[b][:, c * N:(c + 1) * N], tile[:, kk * P:(kk + 1) * P], AT, start=True,
                                       stop=True)
                    ins.then_inc(full[b], 1)

            def transpose_result(name, i, halves=(0, 1)):
                for j in halves:
                    wait_drained((i, j))
                    transpose(name, ev[:, i % 2, :], j)

            def compare_pairs(name, p):
                c0, c1 = PIECES[p]
                b = refill((name, p % 2))
                o = psum[b][0:N, 0:(c1 - c0) * N]
                for n in range(2):
                    t.matmul(o, ones_b[:, :], diag[:, n, c0:c1, :].rearrange("p c n -> p (c n)"), start=(n == 0),
                             stop=False)
                t.matmul(o.rearrange("p (c n) -> p c n", n=N), ident_b[:, :],
                         tri_b[:, :].unsqueeze(1).to_broadcast([N, c1 - c0, N]), start=False, stop=True)\
                    .then_inc(full[b], 1)

            def pair_keys(name, p):
                c0, c1 = PIECES[p]
                b = refill((name, p % 2))
                for c in range(c0, c1):
                    ins = t.matmul(psum[b][0:N, (c - c0) * N:(c - c0 + 1) * N], oh_src[:, c, :], oh_key[:, c, :],
                                   start=True, stop=True)
                ins.then_inc(full[b], 1)

            pe.wait_ge(warm_ready, 1)
            keep_warm("h0T")
            pe.wait_ge(scaled, 1)
            aggregate("h0T", h, scaled_m[:, :], layer=0)
            keep_warm("eqA")
            product(Q, 0, "h0T", end=2, last=False, opens=True)
            keep_warm("eqA", 1)
            product(Q, 0, "h0T", begin=2, end=4, last=False)
            pe.wait_ge(sel_ready, 1)
            pe.wait_ge(bias_lo, 1)
            bias(Q, opens=False)
            product(Q, 0, "h0T", begin=4, end=5, last=False)
            bias(K)
            product(Q, 0, "h0T", begin=5, tail=1)
            pe.wait_ge(ident_ready, 1)
            product(K, 0, "h0T", end=2, last=False)
            pe.wait_ge(diag_ready, 2)
            pe.wait_ge(tri_ready, 1)
            for p in (0, 1):
                compare_pairs("eqA", p)
            product(K, 0, "h0T", begin=2, end=4, last=False)
            for p in (2, 3):
                compare_pairs("eqB", p)
            product(K, 0, "h0T", begin=4, end=6, last=False)
            transpose_result("qT", Q)
            product(K, 0, "h0T", begin=6)
            bias(V)
            product(V, 0, "h0T", end=2, last=False)
            for p, name in enumerate(("eqA", "eqA", "eqB", "eqB")):
                wait_drained((name, p % 2))
            b = refill(("voids", 0))
            for c in range(EC):
                ins = t.matmul(psum[b][0:N, c:c + 1], same[:, c, :], ones_b[:, 0:1], start=True, stop=True)
            ins.then_inc(full[b], 1)
            product(V, 0, "h0T", begin=2, end=6, last=False)
            transpose_result("kT", K)
            product(V, 0, "h0T", begin=6)
            bias(Q2)
            product(Q2, 1, "qT", end=2, last=False)
            pe.wait_ge(onehots_ready, 2 * EC)
            pe.wait_ge(keys_ready, 1)
            for p in (0, 1):
                pair_keys("keyA", p)
            product(Q2, 1, "qT", begin=2, end=3, last=False)
            for p in (2, 3):
                pair_keys("keyB", p)
            product(Q2, 1, "qT", begin=3, end=4, last=False)
            b = refill(("counts", 0))
            for c in range(EC):
                ins = t.matmul(psum[b][0:N, 0:N], oh_src[:, c, :], oh_dst[:, c, :], start=(c == 0), stop=(c == EC - 1))
            ins.then_inc(full[b], 1)
            product(Q2, 1, "qT", begin=4, end=6, last=False)
            transpose_result("vT", V)
            product(Q2, 1, "qT", begin=6)
            bias(K2)
            product(K2, 2, "kT", end=2, last=False)
            wait_drained(("counts", 0))
            b = refill(("countsT", 0))
            t.transpose(psum[b][0:N, 0:N], C[:, 0, :], ident[:, :]).then_inc(full[b], 1)
            product(K2, 2, "kT", begin=2, end=4, last=False)
            wait_drained(("countsT", 0))
            b = refill(("degrees", 0))
            for n in range(2):
                t.matmul(psum[b][0:N, n * N:(n + 1) * N], ones[:, :], C[:, n, :], start=True, stop=True)
                ins = t.matmul(psum[b][0:N, 2 * N + n:2 * N + n + 1], C[:, n, :], ones[:, 0:1], start=True, stop=True)
            ins.then_inc(full[b], 1)
            product(K2, 2, "kT", begin=4, end=6, last=False)
            transpose_result("q2T", Q2)
            product(K2, 2, "kT", begin=6)
            bias(V2)
            product(V2, 0, "vT", end=2, last=False)
            transpose_result("k2T", K2)
            product(V2, 0, "vT", begin=2, end=3, last=False)
            pe.wait_ge(mask_ready, 1)
            for e in range(2):
                wait_drained(("q2T", e))
                wait_drained(("k2T", e))
                for j in range(2):
                    b = refill((f"scores{e}", j))
                    for n in range(2):
                        t.matmul(tview(b, N), ident_r[:, :], mask_parts[:, n, :].unsqueeze(1).to_broadcast([N, HC, N]),
                                 start=(n == 0), stop=False)
                    for c in range(HC):
                        rows, kk = slice(DH * j, DH * j + DH), HC * e + c
                        ins = t.matmul(psum[b][0:N, c * N:(c + 1) * N], q2T[rows, kk, :], k2T[rows, kk, :],
                                       start=False, stop=(c == HC - 1))
                    ins.then_inc(full[b], 1)
            product(V2, 0, "vT", begin=3, end=6, last=False)
            for p in range(4):
                if p == 2:
                    product(V2, 0, "vT", begin=6)
                name = f"probsT{p // 2}"
                pe.wait_ge(probs_ready, p + 1)
                b = refill((name, p % 2))
                for c in range(4):
                    ins = t.transpose(psum[b][0:N, c * N:(c + 1) * N], S[:, 4 * p + c, :], ident[:, :])
                ins.then_inc(full[b], 1)
            for e in range(2):
                wait_drained((V2, e))
                for j in range(2):
                    wait_drained((f"probsT{e}", j))
                b = refill(("headsT", e))
                for c in range(HC):
                    for j in range(2):
                        head = 2 * (HC * e + c) + j
                        ins = t.matmul(psum[b][DH * j:DH * j + DH, c * N:(c + 1) * N],
                                       ev[:, V2 % 2, head * DH:(head + 1) * DH], PT[:, 8 * e + 4 * j + c, :],
                                       start=True, stop=True)
                ins.then_inc(full[b], 1)
                if e == 0:
                    bias(O)
            product(O, 1, "headsT")
            bias(SAGE0)
            residual(SAGE1, 1, opens=True)
            pe.wait_ge(scaled, 2)
            aggregate("mean1T", h, scaled_m[:, :], layer=1)
            for j in range(2):
                pe.wait_ge(h_scaled, j + 1)
                transpose("h1T", h_std, j)
            product(SAGE0, 0, "mean1T", last=False)
            pe.wait_ge(A23_ready, 1)
            b = refill(("rowsum", 0))
            t.matmul(psum[b][0:12, 0:N], bcol[:, :], A2T[:, :], start=True, stop=True).then_inc(full[b], 1)
            product(SAGE0, 2, "h1T", first=4)
            transpose_result("hiddenT", SAGE0, (0,))
            bias(SAGE1, opens=False)
            transpose_result("hiddenT", SAGE0, (1,))
            aggregate("mean2T", ev[:, SAGE0 % 2, :], A1T[:, :])
            product(SAGE1, 1, "hiddenT", last=False)
            product(SAGE1, 2, "mean2T", first=4)
            bias(GCN2)
            residual(GCN2, 2, opens=False)
            pe.wait_ge(scaled, 3)
            aggregate("h2T", h, scaled_m[:, :], layer=2)
            product(GCN2, 0, "h2T")
            bias(GCN3A)
            residual(GCN3B, 3, opens=True)
            pe.wait_ge(scaled, 4)
            aggregate("h3T", h, scaled_m[:, :], layer=3)
            b = FILL[GCN3A, 0][0]
            for e in range(2):
                g = 2 * FIRST_UNIT[GCN3A] + e
                wait_split(g)
                wait_high(("h3T", e))
                for n, (lhs, rhs) in enumerate(((a_hi, w_hi), (a_hi, w_lo), (a_lo, w_hi))):
                    if n == 2:
                        wait_drained(("h3T", e))
                    for q in range(HC):
                        ins = t.matmul(psum[b][0:N, 0:F], lhs[:, 1, HC * e + q, :],
                                       rhs[:, g % RING, q * F:(q + 1) * F], start=False,
                                       stop=(e == 1 and n == 2 and q == HC - 1))
            ins.then_inc(full[b], 1)
            bias(GCN3B, opens=False)
            wait_drained((GCN3A, 0))
            aggregate("gT", ev[:, GCN3A % 2, :], A3T[:, :], 1, 2)
            for k in range(2):
                wait_split(2 * FIRST_UNIT[GCN3B] + k)
            wait_high(("gT", 0))
            for j in range(2):
                b = FILL[GCN3B, j][0]
                for n, (lhs, rhs) in enumerate(((a_hi, w_hi), (a_hi, w_lo), (a_lo, w_hi))):
                    if n == 2:
                        wait_drained(("gT", 0))
                    for k in range(2):
                        r = (2 * FIRST_UNIT[GCN3B] + k) % RING
                        ins = t.matmul(psum[b][0:N, :], lhs[:, 2, k, :], rhs[:, r, hcols(j)], start=False,
                                       stop=(k == 1 and n == 2))
                ins.then_inc(full[b], 1)


WEIGHTS = [("L0_gnn_wq", True), ("L0_gnn_wk", True), ("L0_gnn_wv", True), ("L0_gnn_wiq", True), ("L0_gnn_wik", True),
           ("L0_gnn_wiv", True), ("L0_gnn_wo", True), ("L1_gnn_W_neigh0", False), ("L1_gnn_W_self0", False),
           ("L1_gnn_W_self1", False), ("L1_gnn_W_neigh1", False), ("L2_gnn_W", True), ("L3_gnn_W1", False),
           ("L3_gnn_W2", False)]
BIASES = ["L0_gnn_bq", "L0_gnn_bk", "L0_gnn_bv", "L0_gnn_biq", "L0_gnn_bik", "L0_gnn_biv", "L0_gnn_bo", "L1_gnn_b0",
          "L1_gnn_b1", "L2_gnn_b", "L3_gnn_b1", "L3_gnn_b2"]


def kernel(**inputs):
    import numpy as np
    import concourse.bacc as bacc
    from concourse.bass_utils import run_bass_kernel_spmd

    units = []
    for name, transposed in WEIGHTS:
        w = np.asarray(inputs[name])
        w = w.T if transposed else w
        rows, cols = w.shape
        per = UNIT // cols
        w = w.reshape(rows // (per * P), per, P, cols).transpose(0, 2, 1, 3)
        units.append(w.reshape(-1, P, UNIT))
    biases = np.zeros((12, D), np.float32)
    for n, name in enumerate(BIASES):
        b = np.asarray(inputs[name])
        biases[n, :b.shape[0]] = b
    edges = np.stack([np.asarray(inputs[k]).reshape(EC, N).T for k in ("src", "dst", "edge_type_5")], axis=1)
    arrays = {
        "x": np.ascontiguousarray(inputs["x"]), "weights": np.concatenate(units), "biases": biases,
        "edges": np.ascontiguousarray(edges), "edge_w": np.asarray(inputs["L0_gnn_edge_type_weights"]).reshape(1, 4),
    }
    nc = bacc.Bacc("TRN2", target_bir_lowering=False, num_devices=1)
    args = [nc.dram_tensor(f"in_{k}", a.shape, mybir.dt.from_np(a.dtype), kind="ExternalInput").ap()
            for k, a in arrays.items()]
    args.append(nc.dram_tensor("out_x", (N, D), mybir.dt.float32, kind="ExternalOutput").ap())
    gnn_kernel(nc, *args)
    r = run_bass_kernel_spmd(nc, [{f"in_{k}": a for k, a in arrays.items()}], core_ids=[0])
    return r.results[0]["out_x"]
```
